# Optimizing a Trainium2 kernel written in Bass

```python
import numpy as np
import jax
import jax.numpy as jnp

def _softmax(x, axis=-1):
    return jax.nn.softmax(x, axis=axis)

def _gelu(x):
    return jax.nn.gelu(x, approximate=True)

def _silu(x):
    return jax.nn.silu(x)

def _sigmoid(x):
    return jax.nn.sigmoid(x)

def _layernorm(x, axis=-1, eps=1e-05):
    m = jnp.mean(x, axis=axis, keepdims=True)
    v = jnp.var(x, axis=axis, keepdims=True)
    return (x - m) / jnp.sqrt(v + eps)

def _scatter_add(tgt, idx, src, axis=0):
    return tgt.at[idx].add(src)

def _segment_sum(src, seg, n):
    return jax.ops.segment_sum(src, seg, n)
kernel_name = 'mk_early_fusion_d1_tok_img512_r4_ea23ac'

def setup_inputs(seed: int=0):
    np.random.seed(seed)
    _w = jnp.asarray

    def _rec_inputs():
        import jax
        import jax.numpy as jnp
        _rk = jax.random.key(seed)
        x = -0.000356955 + 1 * jax.random.normal(jax.random.fold_in(_rk, 1), (32, 3, 224, 224), jnp.float32)
        txt = 0.0185972 + 1.43333 * jax.random.normal(jax.random.fold_in(_rk, 2), (32, 77, 128), jnp.float32)
        return (x, txt)
    x, txt = _rec_inputs()

    def _L0_tok_setup():
        import jax, jax.numpy as jnp
        import numpy as np
        key = jax.random.key(seed)
        k1, k2, k3 = jax.random.split(key, 3)
        B, C, H, W = (128, 3, 224, 224)
        E, p = (128, 16)
        K = C * p * p
        img = jax.random.normal(k1, (B, C, H, W), dtype=jnp.float32)
        w = jax.random.normal(k2, (E, K), dtype=jnp.float32) * (1.0 / np.sqrt(K))
        b = jax.random.normal(k3, (E,), dtype=jnp.float32)
        return {'img': img, 'w': w, 'b': b, 'patch_size': p}
    _L0_tok_all = _L0_tok_setup()
    _L0_tok_in = {k: v for k, v in _L0_tok_all.items() if k in ('w', 'b')}
    del _L0_tok_all

    def _L0_attn_setup():
        import jax, jax.numpy as jnp
        import numpy as np
        CHUNK = 64
        THETA = 10000.0

        def rope2d(x):
            b, h, n, d = x.shape
            pad = -n % CHUNK
            if pad:
                x = jnp.pad(x, ((0, 0), (0, 0), (0, pad), (0, 0)))
            c = (n + pad) // CHUNK
            x = x.reshape(b, h, c, CHUNK, d)
            inv = 1.0 / THETA ** (jnp.arange(0, d, 4, dtype=jnp.float32) / d)
            fl = jnp.arange(CHUNK, dtype=jnp.float32)[:, None] * inv[None, :]
            cos_l, sin_l = (jnp.cos(fl), jnp.sin(fl))
            fc = jnp.arange(c, dtype=jnp.float32)[:, None] * inv[None, :]
            cos_c, sin_c = (jnp.cos(fc)[:, None, :], jnp.sin(fc)[:, None, :])
            x1, x2, x3, x4 = jnp.split(x, 4, axis=-1)
            r1 = x1 * cos_l - x2 * sin_l
            r2 = x1 * sin_l + x2 * cos_l
            r3 = x3 * cos_c - x4 * sin_c
            r4 = x3 * sin_c + x4 * cos_c
            out = jnp.concatenate([r1, r2, r3, r4], axis=-1).reshape(b, h, c * CHUNK, d)
            return out[:, :, :n]
        key = jax.random.key(seed)
        ks = jax.random.split(key, 6)
        dim, heads = (128, 8)
        b, n = (2, 512)
        s = 0.02
        return {'x': jax.random.normal(ks[0], (b, n, dim), dtype=jnp.float32), 'w_qkv': jax.random.normal(ks[1], (3 * dim, dim), dtype=jnp.float32) * s, 'b_qkv': jnp.zeros((3 * dim,), dtype=jnp.float32), 'w_pre': jax.random.normal(ks[2], (heads, heads), dtype=jnp.float32) * 0.3, 'w_post': jax.random.normal(ks[3], (heads, heads), dtype=jnp.float32) * 0.3, 'w_out': jax.random.normal(ks[4], (dim, dim), dtype=jnp.float32) * s, 'b_out': jnp.zeros((dim,), dtype=jnp.float32)}
    _L0_attn_all = _L0_attn_setup()
    _L0_attn_in = {k: v for k, v in _L0_attn_all.items() if k in ('w_qkv', 'b_qkv', 'w_pre', 'w_post', 'w_out', 'b_out')}
    del _L0_attn_all

    def _L0_ffn_setup():
        import jax, jax.numpy as jnp
        import numpy as np
        EPS = 1e-05
        TOP_K = 2

        def layer_norm(x, g, b):
            m = x.mean(-1, keepdims=True)
            v = ((x - m) ** 2).mean(-1, keepdims=True)
            return (x - m) / jnp.sqrt(v + EPS) * g + b
        key = jax.random.key(seed)
        ks = jax.random.split(key, 8)
        B, S, D, E, H = (8, 128, 128, 8, 512)
        x = jax.random.normal(ks[0], (B, S, D), dtype=jnp.float32)
        Wg = jax.random.normal(ks[1], (D, E), dtype=jnp.float32) * 0.02
        W1 = jax.random.normal(ks[2], (E, D, H), dtype=jnp.float32) * 0.02
        b1 = jnp.zeros((E, H), dtype=jnp.float32)
        W2 = jax.random.normal(ks[3], (E, H, D), dtype=jnp.float32) * 0.02
        b2 = jnp.zeros((E, D), dtype=jnp.float32)
        ln_g = jnp.ones((D,), dtype=jnp.float32)
        ln_b = jnp.zeros((D,), dtype=jnp.float32)
        out_g = jnp.ones((D,), dtype=jnp.float32)
        out_b = jnp.zeros((D,), dtype=jnp.float32)
        return {'x': x, 'Wg': Wg, 'W1': W1, 'b1': b1, 'W2': W2, 'b2': b2, 'ln_g': ln_g, 'ln_b': ln_b, 'out_g': out_g, 'out_b': out_b}
    _L0_ffn_all = _L0_ffn_setup()
    _L0_ffn_in = {k: v for k, v in _L0_ffn_all.items() if k in ('Wg', 'W1', 'b1', 'W2', 'b2', 'ln_g', 'ln_b', 'out_g', 'out_b')}
    del _L0_ffn_all
    return {'x': x, 'txt': txt, 'L0_tok_w': _L0_tok_in['w'], 'L0_tok_b': _L0_tok_in['b'], 'L0_attn_w_qkv': _L0_attn_in['w_qkv'], 'L0_attn_b_qkv': _L0_attn_in['b_qkv'], 'L0_attn_w_pre': _L0_attn_in['w_pre'], 'L0_attn_w_post': _L0_attn_in['w_post'], 'L0_attn_w_out': _L0_attn_in['w_out'], 'L0_attn_b_out': _L0_attn_in['b_out'], 'L0_ffn_Wg': _L0_ffn_in['Wg'], 'L0_ffn_W1': _L0_ffn_in['W1'], 'L0_ffn_b1': _L0_ffn_in['b1'], 'L0_ffn_W2': _L0_ffn_in['W2'], 'L0_ffn_b2': _L0_ffn_in['b2'], 'L0_ffn_ln_g': _L0_ffn_in['ln_g'], 'L0_ffn_ln_b': _L0_ffn_in['ln_b'], 'L0_ffn_out_g': _L0_ffn_in['out_g'], 'L0_ffn_out_b': _L0_ffn_in['out_b']}

def reference(x, txt, L0_tok_w, L0_tok_b, L0_attn_w_qkv, L0_attn_b_qkv, L0_attn_w_pre, L0_attn_w_post, L0_attn_w_out, L0_attn_b_out, L0_ffn_Wg, L0_ffn_W1, L0_ffn_b1, L0_ffn_W2, L0_ffn_b2, L0_ffn_ln_g, L0_ffn_ln_b, L0_ffn_out_g, L0_ffn_out_b):
    import jax
    import jax.numpy as jnp

    def _L0_tok_ref(img, w, b, patch_size):
        import jax, jax.numpy as jnp
        import numpy as np
        B, C, H, W = img.shape
        p = patch_size
        Hp, Wp = (H // p, W // p)
        S = Hp * Wp
        patches = img.reshape(B, C, Hp, p, Wp, p)
        patches = patches.transpose(0, 2, 4, 1, 3, 5).reshape(B, S, C * p * p)
        out = jnp.einsum('bsk,ek->bse', patches, w) + b
        return out

    def _L0_attn_ref(x, w_qkv, b_qkv, w_pre, w_post, w_out, b_out):
        import jax, jax.numpy as jnp
        import numpy as np
        CHUNK = 64
        THETA = 10000.0

        def rope2d(x):
            b, h, n, d = x.shape
            pad = -n % CHUNK
            if pad:
                x = jnp.pad(x, ((0, 0), (0, 0), (0, pad), (0, 0)))
            c = (n + pad) // CHUNK
            x = x.reshape(b, h, c, CHUNK, d)
            inv = 1.0 / THETA ** (jnp.arange(0, d, 4, dtype=jnp.float32) / d)
            fl = jnp.arange(CHUNK, dtype=jnp.float32)[:, None] * inv[None, :]
            cos_l, sin_l = (jnp.cos(fl), jnp.sin(fl))
            fc = jnp.arange(c, dtype=jnp.float32)[:, None] * inv[None, :]
            cos_c, sin_c = (jnp.cos(fc)[:, None, :], jnp.sin(fc)[:, None, :])
            x1, x2, x3, x4 = jnp.split(x, 4, axis=-1)
            r1 = x1 * cos_l - x2 * sin_l
            r2 = x1 * sin_l + x2 * cos_l
            r3 = x3 * cos_c - x4 * sin_c
            r4 = x3 * sin_c + x4 * cos_c
            out = jnp.concatenate([r1, r2, r3, r4], axis=-1).reshape(b, h, c * CHUNK, d)
            return out[:, :, :n]
        b, n, dim = x.shape
        heads = w_pre.shape[0]
        d = dim // heads
        scale = d ** (-0.5)
        qkv = x @ w_qkv.T + b_qkv
        q, k, v = jnp.split(qkv, 3, axis=-1)

        def to_heads(t):
            return t.reshape(b, n, heads, d).transpose(0, 2, 1, 3)
        q, k, v = (to_heads(q), to_heads(k), to_heads(v))
        q = rope2d(q)
        k = rope2d(k)
        logits = jnp.einsum('bhid,bhjd->bhij', q, k) * scale
        logits = jnp.einsum('bhij,gh->bgij', logits, w_pre)
        attn = jax.nn.softmax(logits, axis=-1)
        attn = jnp.einsum('bhij,gh->bgij', attn, w_post)
        out = jnp.einsum('bhij,bhjd->bhid', attn, v)
        out = out.transpose(0, 2, 1, 3).reshape(b, n, dim)
        return out @ w_out.T + b_out

    def _L0_ffn_ref(x, Wg, W1, b1, W2, b2, ln_g, ln_b, out_g, out_b):
        import jax, jax.numpy as jnp
        import numpy as np
        EPS = 1e-05
        TOP_K = 2

        def layer_norm(x, g, b):
            m = x.mean(-1, keepdims=True)
            v = ((x - m) ** 2).mean(-1, keepdims=True)
            return (x - m) / jnp.sqrt(v + EPS) * g + b
        xn = layer_norm(x, ln_g, ln_b)
        logits = jnp.einsum('bsd,de->bse', xn, Wg)
        probs = jax.nn.softmax(logits, axis=-1)
        top_p, top_i = jax.lax.top_k(probs, TOP_K)
        conf = top_p / top_p.sum(-1, keepdims=True)
        h = jax.nn.gelu(jnp.einsum('bsd,edh->bseh', xn, W1) + b1)
        o = jnp.einsum('bseh,ehd->bsed', h, W2) + b2
        sel = jnp.take_along_axis(o, top_i[..., None], axis=2)
        combined = jnp.einsum('bskd,bsk->bsd', sel, conf)
        return layer_norm(x + combined, out_g, out_b)
    h = _L0_tok_ref(x, L0_tok_w, L0_tok_b, 16)
    h = jnp.concatenate([h, txt], axis=1)
    h = h + _L0_attn_ref(_layernorm(h, axis=-1), L0_attn_w_qkv, L0_attn_b_qkv, L0_attn_w_pre, L0_attn_w_post, L0_attn_w_out, L0_attn_b_out)
    h = h + _L0_ffn_ref(_layernorm(h, axis=-1), L0_ffn_Wg, L0_ffn_W1, L0_ffn_b1, L0_ffn_W2, L0_ffn_b2, L0_ffn_ln_g, L0_ffn_ln_b, L0_ffn_out_g, L0_ffn_out_b)
    return h

_drawn_inputs = setup_inputs


def setup_inputs(seed=0):
    import zlib

    import numpy as np

    out = dict(_drawn_inputs(seed))
    spreads = {'L0_attn_b_qkv': (0.0, 0.57),
     'L0_attn_b_out': (0.0, 0.1),
     'L0_ffn_b1': (0.0, 0.8),
     'L0_ffn_b2': (0.0, 0.282),
     'L0_ffn_ln_g': (1.0, 0.6),
     'L0_ffn_ln_b': (0.0, 0.7),
     'L0_ffn_out_g': (1.0, 0.2),
     'L0_ffn_out_b': (0.0, 0.1)}
    factors = {'L0_attn_w_qkv': 3.04,
     'L0_attn_w_pre': 8.0,
     'L0_attn_w_post': 2.973,
     'L0_ffn_W1': 3.331,
     'L0_ffn_W2': 3.109}
    for name, (base, spread) in spreads.items():
        noise = np.random.default_rng([zlib.crc32(name.encode()), seed]).standard_normal(out[name].shape)
        drawn = base * np.exp(spread * noise) if base else spread * noise
        out[name] = jnp.asarray(drawn.astype(out[name].dtype))
    for name, factor in factors.items():
        out[name] = (out[name] * factor).astype(out[name].dtype)
    return out
```

```python
import numpy as np
import concourse.bass as bass
from concourse import mybir
from contextlib import ExitStack

B, C, IMG, P16 = 32, 3, 224, 16
HP = IMG // P16
TXT, D, NH, DH = 77, 128, 8, 16
NE, FH = 8, 512
NPATCH = HP * HP
N = NPATCH + TXT
R = NPATCH // 2
NT = 3
NV = N + N % 2
NP = NT * R
QH = P16 // 2
KR = C * P16 * 2
FC = FH // 128
EPS = 1e-5


def early_fusion_kernel(nc, x, txt, w_tok, w_qkvr, b_qkr, b_v, w_pre, w_post, w_out, b_out, w_gate,
                        w1, b1, w2, b2, ln_g, ln_b, out_g, out_b, rope, ident, iota, sel, out):
    f32, f32r, u32 = mybir.dt.float32, mybir.dt.float32r, mybir.dt.uint32
    ALU, ACT, AX = mybir.AluOpType, mybir.ActivationFunctionType, mybir.AxisListType
    ctx = ExitStack()
    with ctx:
        def sb(name, shape, dt=f32):
            return ctx.enter_context(nc.sbuf_tensor(name, shape, dt))

        def sem(name):
            return ctx.enter_context(nc.semaphore(name))

        wtok = sb("wtok", [KR + 1, QH, D])
        wqkv = sb("wqkv", [D, 5 * D])
        bqk = sb("bqk", [D, 4])
        bv = sb("bv", [R, D])
        wpre = sb("wpre", [D, NH])
        wpost = sb("wpost", [R, NH, D])
        wout = sb("wout", [D, D])
        bout = sb("bout", [R, D])
        wgate = sb("wgate", [D, NE])
        w1hi = sb("w1hi", [D, NE * FH], f32r)
        w1lo = sb("w1lo", [D, NE * FH], f32r)
        b1c = sb("b1c", [128, NE * FC])
        w2s = sb("w2s", [128, NE * FC, D])
        b2d = sb("b2d", [2 * NE, D])
        b2hi = sb("b2hi", [2 * NE, D], f32r)
        b2lo = sb("b2lo", [2 * NE, D], f32r)
        lng = sb("lng", [D, 1])
        lnb = sb("lnb", [D, 1])
        outg = sb("outg", [R, D])
        outb = sb("outb", [R, D])
        cosT = sb("cosT", [D, 2, NP])
        idn = sb("idn", [128, 128])
        iot = sb("iot", [R, NE])
        self32 = sb("self32", [2 * NE, NE, 128])
        selr = sb("selr", [2 * NE, NE, 128], f32r)
        mhalf = sb("mhalf", [R, NT])
        epsT = sb("epsT", [R, NT])
        xt = sb("xt", [KR + 1, HP * IMG])
        H0 = sb("H0", [R, NT, D])
        HB = sb("HB", [R, NT, D])
        bst = sb("bst", [R, NT, 6])
        hold = sb("hold", [R, 1])
        mv1 = sb("mv1", [R, NT, 2])
        rs1 = sb("rs1", [R, NT])
        xn = sb("xn", [R, NT, D])
        xnT = sb("xnT", [D, NP])
        rc = sb("rc", [D, 2, NP])
        rsn = sb("rsn", [D, 2, NP])
        qT = sb("qT", [D, NP])
        kT = sb("kT", [D, NP])
        qg = sb("qg", [D, NH, NP])
        V = sb("V", [R, NT, D])
        VP = sb("VP", [R, NH, NT, D])
        nmax = sb("nmax", [R, NH * NT])
        esum = sb("esum", [R, NH * NT])
        rsum = sb("rsum", [R, NH * NT])
        E = sb("E", [R, 2, NT, NP])
        AT = sb("AT", [R, 2, NT, NP])
        oT = sb("oT", [D, NP])
        H1 = sb("H1", [R, NT, D])
        mv2 = sb("mv2", [R, NT, 2])
        rs2 = sb("rs2", [R, NT])
        tv2 = sb("tv2", [R, NT])
        rr2 = sb("rr2", [R, NT])
        y2 = sb("y2", [R, NT, D])
        xh = sb("xh", [R, NT, D])
        x2T = sb("x2T", [D, NP])
        xhi = sb("xhi", [D, NP], f32r)
        xlo = sb("xlo", [D, NP], f32r)
        gl = sb("gl", [R, NT, NE])
        m8 = sb("m8", [R, NT, 8])
        ix8 = sb("ix8", [R, NT, 8], u32)
        ixf = sb("ixf", [R, NT, 2])
        dl = sb("dl", [R, NT])
        ed = sb("ed", [R, NT])
        ed1 = sb("ed1", [R, NT])
        cf = sb("cf", [R, 2, NT])
        ca = sb("ca", [R, NT, NE])
        cb = sb("cb", [R, NT, NE])
        cc = sb("cc", [R, NT, NE])
        chr_ = sb("chr_", [R, NT, NE], f32r)
        chl = sb("chl", [R, NT, 2 * NE])
        cT = sb("cT", [2 * NE, NP], f32r)
        G = sb("G", [128, 2, FC, N])
        GS = sb("GS", [128, 3, FC, N])
        comb = sb("comb", [D, NP])
        H1b = sb("H1b", [R, NT, D])
        y2b = sb("y2b", [R, NT, D])
        T3 = sb("T3", [R, NT, D])
        mv3 = sb("mv3", [R, NT, 2])
        rs3 = sb("rs3", [R, NT])
        z3 = sb("z3", [R, NT, D])
        fin = sb("fin", [R, NT, D])

        PS = ctx.enter_context(nc.psum_tensor("PS", [128, 8, 512], f32))
        RING = 3
        TB = 3
        ACC = 5
        MA, MB = 6, 7
        acc = PS[:, ACC, 0:N]

        s_wtok, s_wqkv, s_small, s_w1, s_w2 = (sem(n) for n in
                                               ("tok_weights", "qkv_weights", "small_weights", "w1_loaded", "w2_loaded"))
        s_set = sem("setup_gpsimd")
        s_one = sem("ones_row")
        s_wr = sem("weights_rounded")
        s_x, s_txt, s_st = sem("x_loaded"), sem("txt_loaded"), sem("stored")
        s_tok, s_xnT, s_qk, s_v = sem("tok_ps"), sem("xnT_ps"), sem("qk_ps"), sem("v_ps")
        s_h0, s_st1, s_r1, s_xn, s_xnTe = sem("h0"), sem("stats1"), sem("rstd1"), sem("xn"), sem("xnT_sb")
        s_bn = sem("bn_stats")
        s_hb = sem("hb")
        s_rope, s_qk_sb, s_qg, s_vb, s_vp = sem("rope"), sem("qk_sb"), sem("qg"), sem("vb"), sem("vp")
        s_lg, s_max, s_exp, s_rec, s_nrm = sem("scores_ps"), sem("max"), sem("exp"), sem("recip"), sem("probs")
        s_tr, s_at, s_av, s_ot = sem("probsT_ps"), sem("probsT_sb"), sem("av_ps"), sem("attn_sb")
        s_proj, s_h1, s_st2, s_r2, s_y2, s_xh = (sem(n) for n in ("proj_ps", "h1", "stats2", "rstd2", "y2", "xhat"))
        s_p2 = sem("rstd2_steps")
        s_x2T, s_x2Te, s_gate, s_gl, s_m8, s_dl = (sem(n) for n in
                                                  ("x2T_ps", "x2T_sb", "gate_ps", "gate_sb", "top8", "logit_gap"))
        s_ed, s_c, s_chl, s_cTp, s_cT = sem("gap_exp"), sem("conf_steps"), sem("conf_hl"), sem("cT_ps"), sem("cT_sb")
        s_xhi, s_xhl = sem("xhi"), sem("xhl")
        s_cb, s_l1, s_ge, s_sc, s_l2 = sem("conf_ps"), sem("hidden_ps"), sem("gelu"), sem("scaled"), sem("l2_done")
        s_comb, s_cmT, s_t3, s_st3, s_r3, s_fin = (sem(n) for n in
                                                  ("comb_sb", "combT_ps", "t3", "stats3", "rstd3", "fin"))
        s_p1, s_p3, s_z = sem("rstd1_steps"), sem("rstd3_steps"), sem("z_steps")
        s_cp = sem("kept")

        block = ctx.enter_context(nc.Block())

        def steps(eng, step):
            step(0)
            step(1)
            with eng.Fori(2, B - 1) as i:
                step(i, True)
            step(B - 1)
            step(B)
            step(B + 1)

        def parts(i, full):
            if full:
                return True, True, True, True
            return i < B, 1 <= i <= B, i >= 2, i < B - 1

        @block.sync
        def _(sp):
            sp.dma_start(wtok[:], w_tok).then_inc(s_wtok, 16)

            def load(b, first=False):
                if not first:
                    sp.wait_ge(s_tok, b)
                for half in range(2):
                    for c in range(C):
                        r0 = half * C * P16 + c * P16
                        dst = xt[r0:r0 + P16, :].rearrange("p (h w) -> p h w", w=IMG)[:, :, 0:IMG - QH * half]
                        src = x[b, c].rearrange("(h p) w -> p h w", p=P16)[:, :, QH * half:IMG]
                        sp.dma_start(dst, src).then_inc(s_x, 16)
                if not first:
                    sp.wait_ge(s_xn, b)
                    sp.wait_ge(s_hb, b)
                else:
                    sp.wait_ge(s_set, 4)
                sp.dma_start(H0[0:TXT, 2, :], txt[b]).then_inc(s_txt, 16)

            def store(k):
                sp.wait_ge(s_fin, k + 1)
                for t in range(2):
                    sp.dma_start(out[k, t * R:(t + 1) * R, :], fin[:, t, :]).then_inc(s_st, 16)
                sp.dma_start(out[k, NPATCH:N, :], fin[0:TXT, 2, :]).then_inc(s_st, 16)

            load(0, True)
            sp.dma_start(wqkv[:], w_qkvr).then_inc(s_wqkv, 16)
            sp.dma_start(cosT[:], rope).then_inc(s_wqkv, 16)
            sp.dma_start(bqk[:], b_qkr).then_inc(s_wqkv, 16)
            for dst, src in ((bv, b_v), (wpre, w_pre), (wpost, w_post), (wout, w_out), (bout, b_out),
                             (wgate, w_gate), (b1c, b1), (b2d, b2), (lng, ln_g), (lnb, ln_b), (outg, out_g),
                             (outb, out_b), (idn, ident), (iot, iota), (self32, sel)):
                sp.dma_start(dst[:], src).then_inc(s_small, 16)

            def step(i, full=False):
                attn, rout, outp, emb = parts(i, full)
                if emb:
                    load(i + 1)
                if outp:
                    store(i - 2)
            steps(sp, step)
            sp.wait_ge(s_st, 48 * B)

        NSMALL = 15

        @block.gpsimd
        def _(pool):
            nc.gpsimd.memset(H0[:], 0.0).then_inc(s_set, 1)
            nc.gpsimd.memset(E[:], 0.0).then_inc(s_set, 1)
            nc.gpsimd.memset(oT[:], 0.0).then_inc(s_set, 1)
            nc.gpsimd.memset(comb[:], 0.0).then_inc(s_set, 1)
            nc.gpsimd.memset(mhalf[:], -0.5)
            nc.gpsimd.memset(epsT[:], EPS).then_inc(s_set, 1)
            pool.wait_ge(s_small, 16 * NSMALL)
            nc.gpsimd.tensor_scalar(wpre[:], wpre[:], DH ** -0.5, None, ALU.mult).then_inc(s_set, 1)

            def rstd(mv, dst, sem_steps, sem_done, n, k):
                nc.gpsimd.tensor_tensor(dst[:], mv[:, :, 1], epsT[:], ALU.add).then_inc(sem_steps, 1)
                pool.wait_ge(sem_steps, n)
                nc.gpsimd.tensor_tensor(dst[:], dst[:], mhalf[:], ALU.pow).then_inc(sem_done, 1)

            def norm1(b):
                pool.wait_ge(s_st1, b + 1)
                rstd(mv1, rs1, s_p1, s_r1, b + 1, 0)

            def hb(b, first=False):
                pool.wait_ge(s_h0, b + 1)
                pool.wait_ge(s_txt, 16 * (b + 1))
                if not first:
                    pool.wait_ge(s_h1, b)
                nc.gpsimd.tensor_tensor(HB[:], H0[:], bout[:].unsqueeze(1).broadcast_to([R, NT, D]),
                                        ALU.add).then_inc(s_hb, 1)

            def rope_add(b, n):
                pool.wait_ge(s_rope, 4 * b + 2 * n + 2)
                if n == 0:
                    dst = qT
                else:
                    dst = kT
                nc.gpsimd.tensor_tensor(dst[:], rc[:, n, :], rsn[:, n, :], ALU.add).then_inc(s_qk_sb, 1)

            def vpost(b):
                pool.wait_ge(s_vb, b + 1)
                for h in range(NH):
                    nc.gpsimd.tensor_tensor(VP[:, h, :, :], V[:], wpost[:, h, :].unsqueeze(1).broadcast_to([R, NT, D]),
                                            ALU.mult).then_inc(s_vp, 1)

            def norm2(b):
                pool.wait_ge(s_st2, b + 1)
                rstd(mv2, rs2, s_p2, s_r2, 4 * b + 1, 0)
                pool.wait_ge(s_r2, b + 1)
                nc.gpsimd.tensor_tensor(tv2[:], mv2[:, :, 1], rs2[:], ALU.mult).then_inc(s_p2, 1)
                pool.wait_ge(s_p2, 4 * b + 2)
                nc.gpsimd.tensor_tensor(tv2[:], tv2[:], rs2[:], ALU.mult).then_inc(s_p2, 1)
                pool.wait_ge(s_p2, 4 * b + 3)
                nc.gpsimd.tensor_tensor(tv2[:], tv2[:], epsT[:], ALU.add).then_inc(s_p2, 1)
                pool.wait_ge(s_p2, 4 * b + 4)
                nc.gpsimd.tensor_tensor(rr2[:], tv2[:], mhalf[:], ALU.pow)
                for t in range(NT):
                    last = nc.gpsimd.tensor_scalar(y2[:, t, :], H1[:, t, :], mv2[:, t, 0:1], rs2[:, t:t + 1],
                                                   ALU.subtract, ALU.mult)
                last.then_inc(s_y2, 1)
                pool.wait_ge(s_set, 5)
                pool.wait_ge(s_y2, b + 1)
                for t in range(NT):
                    last = nc.gpsimd.tensor_scalar(xh[:, t, :], y2[:, t, :], rr2[:, t:t + 1], None, ALU.mult)
                last.then_inc(s_xh, 1)

            def output(k, first):
                pool.wait_ge(s_st3, k + 1)
                rstd(mv3, rs3, s_p3, s_r3, k + 1, 0)
                pool.wait_ge(s_set, 5)
                pool.wait_ge(s_r3, k + 1)
                for t in range(NT):
                    last = nc.gpsimd.tensor_scalar(z3[:, t, :], T3[:, t, :], mv3[:, t, 0:1], rs3[:, t:t + 1],
                                                   ALU.subtract, ALU.mult)
                last.then_inc(s_z, 1)
                pool.wait_ge(s_z, 3 * k + 1)
                nc.gpsimd.tensor_tensor(z3[:], z3[:], outg[:].unsqueeze(1).broadcast_to([R, NT, D]),
                                        ALU.mult).then_inc(s_z, 1)
                pool.wait_ge(s_z, 3 * k + 2)
                nc.gpsimd.tensor_tensor(z3[:], z3[:], outb[:].unsqueeze(1).broadcast_to([R, NT, D]),
                                        ALU.add).then_inc(s_z, 1)
                pool.wait_ge(s_z, 3 * k + 3)
                if not first:
                    pool.wait_ge(s_st, 48 * k)
                nc.gpsimd.tensor_tensor(fin[:], z3[:], H1b[:], ALU.add).then_inc(s_fin, 1)

            def keep(j, first):
                pool.wait_ge(s_set, 5)
                if not first:
                    pool.wait_ge(s_t3, j)
                    pool.wait_ge(s_fin, j)
                nc.gpsimd.tensor_copy(y2b[:], y2[:])
                nc.gpsimd.tensor_copy(H1b[:], H1[:]).then_inc(s_cp, 1)

            norm1(0)
            hb(0, True)
            rope_add(0, 0)
            rope_add(0, 1)
            vpost(0)

            def step(i, full=False):
                attn, rout, outp, emb = parts(i, full)
                if outp:
                    output(i - 2, not full and i == 2)
                if rout:
                    keep(i - 1, not full and i == 1)
                if emb:
                    norm1(i + 1)
                if attn:
                    norm2(i)
                if emb:
                    hb(i + 1)
                    rope_add(i + 1, 0)
                    rope_add(i + 1, 1)
                    vpost(i + 1)
            steps(pool, step)

        @block.scalar
        def _(act):
            act.dma_start(GS[:, 0:2, :, :].rearrange("p a c n -> p (a c n)")[:, 0:2048], w1[:, 0:2048]).then_inc(s_w1, 16)
            act.dma_start(G[:].rearrange("p a c n -> p (a c n)")[:, 0:2048], w1[:, 2048:4096]).then_inc(s_w1, 16)
            act.dma_start(w2s[:], w2).then_inc(s_w2, 16)

            def probs(i, g):
                for t in range(NT):
                    n = NT * g + t
                    act.wait_ge(s_max, NH * NT * i + n + 1)
                    if t == 0:
                        if g >= 2:
                            act.wait_ge(s_tr, NH * NT * i + NT * (g - 1))
                        elif isinstance(i, int) and i == 0:
                            act.wait_ge(s_set, 6)
                        else:
                            act.wait_ge(s_tr, NH * NT * (i - 1) + NT * (NH + g - 1))
                    nc.scalar.activation(E[:, g % 2, t, 0:N], PS[0:R, t, 0:N], ACT.Exp, bias=nmax[:, n:n + 1],
                                         accum_out=esum[:, n:n + 1]).then_inc(s_exp, 1)

            def probsT(i, g):
                for t in range(NT):
                    n = NT * g + t
                    act.wait_ge(s_tr, NH * NT * i + n + 1)
                    if t == 0:
                        if g >= 2:
                            act.wait_ge(s_av, NH * i + g - 1)
                        elif not (isinstance(i, int) and i == 0):
                            act.wait_ge(s_av, NH * (i - 1) + NH + g - 1)
                    nc.scalar.copy(AT[:, g % 2, t, :], PS[0:R, TB + n % 2, 0:NP]).then_inc(s_at, 1)

            def attn_out(i):
                act.wait_ge(s_av, NH * (i + 1))
                if not (isinstance(i, int) and i == 0):
                    act.wait_ge(s_proj, i)
                nc.scalar.copy(oT[:, 0:N], acc).then_inc(s_ot, 1)

            def step(i, full=False):
                attn, rout, outp, emb = parts(i, full)
                if attn:
                    for g in range(NH):
                        probs(i, g)
                        if g == 0 and rout:
                            act.wait_ge(s_dl, i)
                            nc.scalar.activation(ed[:], dl[:], ACT.Exp).then_inc(s_ed, 1)
                        if g >= 1:
                            probsT(i, g - 1)
                    probsT(i, NH - 1)
                    attn_out(i)
                elif rout:
                    act.wait_ge(s_dl, i)
                    nc.scalar.activation(ed[:], dl[:], ACT.Exp).then_inc(s_ed, 1)
                if rout:
                    j = i - 1
                    for e in range(NE):
                        for c in range(FC):
                            n = FC * e + c
                            act.wait_ge(s_l1, NE * FC * j + n + 1)
                            if c == 0:
                                if e >= 2:
                                    act.wait_ge(s_sc, NE * j + e - 1)
                                elif isinstance(i, int) and i == 1:
                                    act.wait_ge(s_wr, 4)
                                else:
                                    act.wait_ge(s_sc, NE * (j - 1) + NE + e - 1)
                            nc.scalar.activation(G[:, e % 2, c, :], PS[:, n % RING, 0:N], ACT.Gelu_apprx_tanh,
                                                 bias=b1c[:, n:n + 1]).then_inc(s_ge, 1)
            steps(act, step)

        @block.vector
        def _(dve):
            v = nc.vector
            v.memset(xt[KR:KR + 1, :], 1.0).then_inc(s_one, 1)
            dve.wait_ge(s_small, 16 * NSMALL)
            dve.wait_ge(s_w1, 32)
            st = (GS[:, 0:2, :, :].rearrange("p a c n -> p (a c n)")[:, 0:2048],
                  G[:].rearrange("p a c n -> p (a c n)")[:, 0:2048])
            for a in range(2):
                v.tensor_copy(w1hi[:, a * 2048:(a + 1) * 2048], st[a])
            v.tensor_copy(b2hi[:], b2d[:])
            v.tensor_copy(selr[:], self32[:]).then_inc(s_wr, 1)
            dve.wait_ge(s_wr, 1)
            for a in range(2):
                v.tensor_tensor(w1lo[:, a * 2048:(a + 1) * 2048], st[a], w1hi[:, a * 2048:(a + 1) * 2048].bitcast(f32),
                                ALU.subtract).then_inc(s_wr, 1)
            v.tensor_tensor(b2lo[:], b2d[:], b2hi[:].bitcast(f32), ALU.subtract).then_inc(s_wr, 1)

            def stats(src, mv, n, done):
                for t in range(NT):
                    last = v.bn_stats(bst[:, t, :], src[:, t, :])
                last.then_inc(s_bn, 1)
                dve.wait_ge(s_bn, n)
                v.tensor_copy(hold[:], bst[:, 0, 0:1])
                for t in range(NT):
                    last = v.bn_aggr(mv[:, t, :], bst[:, t, :])
                last.then_inc(done, 1)

            def tokens(b, first=False):
                dve.wait_ge(s_tok, b + 1)
                if first:
                    dve.wait_ge(s_set, 5)
                else:
                    dve.wait_ge(s_hb, b)
                v.tensor_copy(H0[:, 0:2, :], PS[0:R, MA, 0:2 * D].rearrange("p (t d) -> p t d", t=2)).then_inc(s_h0, 1)
                dve.wait_ge(s_h0, b + 1)
                dve.wait_ge(s_txt, 16 * (b + 1))
                stats(H0, mv1, count["bn"](b, 1), s_st1)

            def normed(b, first=False):
                dve.wait_ge(s_r1, b + 1)
                if not first:
                    dve.wait_ge(s_xnT, b)
                for t in range(NT):
                    last = v.tensor_scalar(xn[:, t, :], H0[:, t, :], mv1[:, t, 0:1], rs1[:, t:t + 1],
                                           ALU.subtract, ALU.mult)
                last.then_inc(s_xn, 1)

            def normedT(b, first=False):
                dve.wait_ge(s_xnT, b + 1)
                if not first:
                    dve.wait_ge(s_v, b)
                v.tensor_copy(xnT[:], PS[:, MA, 0:NP]).then_inc(s_xnTe, 1)

            def rope_mul(b, n):
                dve.wait_ge(s_qk, 4 * b + 2 * n + 2)
                v.scalar_tensor_tensor(rc[:, n, :], PS[:, MB, 0:NP], bqk[:, 2 * n:2 * n + 1], cosT[:, 0, :],
                                       ALU.add, ALU.mult).then_inc(s_rope, 1)
                v.scalar_tensor_tensor(rsn[:, n, :], PS[:, MA, 0:NP], bqk[:, 2 * n + 1:2 * n + 2], cosT[:, 1, :],
                                       ALU.add, ALU.mult).then_inc(s_rope, 1)

            def values(b):
                dve.wait_ge(s_v, b + 1)
                if not (isinstance(b, int) and b == 0):
                    dve.wait_ge(s_vp, NH * b)
                v.tensor_tensor(V[:], PS[0:R, MB, 0:NT * D].rearrange("p (t d) -> p t d", t=NT),
                                bv[:].unsqueeze(1).broadcast_to([R, NT, D]), ALU.add).then_inc(s_vb, 1)

            def mixed_q(b):
                dve.wait_ge(s_qk_sb, 2 * b + 1)
                if isinstance(b, int) and b == 0:
                    dve.wait_ge(s_set, 6)
                for g in range(NH):
                    v.tensor_scalar(qg[:, g, :], qT[:], wpre[:, g:g + 1], None, ALU.mult).then_inc(s_qg, 1)

            def head_probs(i, g):
                dve.wait_ge(s_exp, NH * NT * i + NT * (g + 1))
                v.reciprocal(rsum[:, NT * g:NT * g + NT], esum[:, NT * g:NT * g + NT]).then_inc(s_rec, 1)
                dve.wait_ge(s_rec, NH * i + g + 1)
                for t in range(NT):
                    last = v.tensor_scalar(E[:, g % 2, t, 0:N], E[:, g % 2, t, 0:N],
                                           rsum[:, NT * g + t:NT * g + t + 1], None, ALU.mult)
                last.then_inc(s_nrm, 1)

            def head_max(i, g):
                for t in range(NT):
                    n = NT * g + t
                    dve.wait_ge(s_lg, NH * NT * i + n + 1)
                    v.tensor_reduce(nmax[:, n:n + 1], PS[0:R, t, 0:N], AX.X, ALU.max, negate=True).then_inc(s_max, 1)

            def router_sum(j):
                dve.wait_ge(s_ed, j + 1)
                v.tensor_scalar(ed1[:], ed[:], 1.0, None, ALU.add).then_inc(s_c, 1)
                v.tensor_copy(ixf[:], ix8[:, :, 0:2])
                dve.wait_ge(s_c, 5 * j + 1)
                v.reciprocal(cf[:, 0, :], ed1[:]).then_inc(s_c, 1)
                dve.wait_ge(s_c, 5 * j + 2)
                v.tensor_tensor(cf[:, 1, :], ed[:], cf[:, 0, :], ALU.mult).then_inc(s_c, 1)
                dve.wait_ge(s_c, 5 * j + 3)
                for t in range(NT):
                    v.tensor_scalar(ca[:, t, :], iot[:], ixf[:, t, 0:1], cf[:, 0, t:t + 1], ALU.is_equal, ALU.mult)
                    last = v.tensor_scalar(cb[:, t, :], iot[:], ixf[:, t, 1:2], cf[:, 1, t:t + 1],
                                           ALU.is_equal, ALU.mult)
                last.then_inc(s_c, 1)
                dve.wait_ge(s_c, 5 * j + 4)
                v.tensor_tensor(cc[:], ca[:], cb[:], ALU.add).then_inc(s_c, 1)
                dve.wait_ge(s_c, 5 * j + 5)
                v.tensor_copy(chr_[:], cc[:]).then_inc(s_chl, 1)
                dve.wait_ge(s_chl, 3 * j + 1)
                v.tensor_copy(chl[:, :, 0:NE], chr_[:].bitcast(f32)).then_inc(s_chl, 1)
                v.tensor_tensor(chl[:, :, NE:2 * NE], cc[:], chr_[:].bitcast(f32), ALU.subtract).then_inc(s_chl, 1)

            def router_T(j):
                dve.wait_ge(s_cTp, j + 1)
                v.tensor_copy(cT[:], PS[0:2 * NE, MB, 0:NP]).then_inc(s_cT, 1)

            def router_top(i):
                dve.wait_ge(s_gate, i + 1)
                v.tensor_copy(gl[:], PS[0:R, MB, 0:NT * NE].rearrange("p (t e) -> p t e", t=NT)).then_inc(s_gl, 1)
                dve.wait_ge(s_one, 1)
                dve.wait_ge(s_gl, i + 1)
                for t in range(NT):
                    last = v.max(m8[:, t, :], gl[:, t, :])
                last.then_inc(s_m8, 1)
                dve.wait_ge(s_one, 1)
                dve.wait_ge(s_m8, i + 1)
                for t in range(NT):
                    v.max_index(ix8[:, t, :], m8[:, t, :], gl[:, t, :])
                v.tensor_tensor(dl[:], m8[:, :, 1], m8[:, :, 0], ALU.subtract).then_inc(s_dl, 1)

            def residual(i):
                dve.wait_ge(s_proj, i + 1)
                dve.wait_ge(s_hb, i + 1)
                if not (isinstance(i, int) and i == 0):
                    dve.wait_ge(s_cp, i)
                v.tensor_tensor(H1[:], PS[0:R, MB, 0:NT * D].rearrange("p (t d) -> p t d", t=NT), HB[:],
                                ALU.add).then_inc(s_h1, 1)
                dve.wait_ge(s_h1, i + 1)
                stats(H1, mv2, count["bn"](i, 2), s_st2)

            def x2_T(i):
                dve.wait_ge(s_x2T, i + 1)
                v.tensor_scalar(x2T[:], PS[:, MA, 0:NP], lng[:], lnb[:], ALU.mult, ALU.add).then_inc(s_x2Te, 1)

            def x2_split(j):
                if isinstance(j, int):
                    if j >= 1:
                        dve.wait_ge(s_l1, NE * FC * j)
                else:
                    dve.wait_ge(s_l1, NE * FC * j)
                v.tensor_copy(xhi[:], x2T[:]).then_inc(s_xhi, 1)
                dve.wait_ge(s_xhi, j + 1)
                v.tensor_tensor(xlo[:], x2T[:], xhi[:].bitcast(f32), ALU.subtract).then_inc(s_xhl, 1)

            def combined(k):
                dve.wait_ge(s_l2, NE * (k + 1))
                v.tensor_copy(comb[:, 0:N], acc).then_inc(s_comb, 1)

            def third(k):
                dve.wait_ge(s_cmT, k + 1)
                dve.wait_ge(s_cp, k + 1)
                v.tensor_tensor(T3[:], PS[0:R, MA, 0:NT * D].rearrange("p (t d) -> p t d", t=NT), y2b[:],
                                ALU.add).then_inc(s_t3, 1)
                dve.wait_ge(s_t3, k + 1)
                stats(T3, mv3, count["bn"](k, 3), s_st3)

            def bn_first(b):
                return 1 if isinstance(b, int) and b == 0 else (2 * b if isinstance(b, int) and b <= 2 else 3 * b - 2)

            def bn_second(i):
                if isinstance(i, int) and i <= 1:
                    return 3 + 2 * i
                if isinstance(i, int) and i == B - 1:
                    return bn_third(B - 3) + 1
                return 3 * i + 2

            def bn_third(k):
                if isinstance(k, int):
                    i = k + 2
                    if i <= B - 1:
                        return 3 * i
                    return 3 * (B - 1) + 1 + (i - (B - 1))
                return 3 * (k + 2)
            count = {"bn": lambda b, which: (bn_first, bn_second, bn_third)[which - 1](b)}

            tokens(0, True)
            normed(0, True)
            normedT(0, True)
            rope_mul(0, 0)
            rope_mul(0, 1)
            values(0)
            mixed_q(0)

            def step(i, full=False):
                attn, rout, outp, emb = parts(i, full)
                j, k = i - 1, i - 2
                if outp:
                    combined(k)
                for g in range(NH):
                    if attn:
                        if g >= 1:
                            head_probs(i, g - 1)
                        head_max(i, g)
                    if g == 2 and outp:
                        third(k)
                    if g == 3 and rout:
                        router_sum(j)
                    if g == 5 and rout:
                        router_T(j)
                    if g == 6 and rout:
                        x2_split(j)
                if attn:
                    head_probs(i, NH - 1)
                for e in range(NE):
                    if e == 0 and emb:
                        tokens(i + 1)
                    if e == 1 and attn:
                        residual(i)
                    if e == 2 and emb:
                        normed(i + 1)
                    if e == 3 and emb:
                        normedT(i + 1)
                    if e == 4 and emb:
                        rope_mul(i + 1, 0)
                    if e == 5 and emb:
                        rope_mul(i + 1, 1)
                    if e == 6:
                        if emb:
                            values(i + 1)
                        if attn:
                            x2_T(i)
                    if e == 7 and emb:
                        mixed_q(i + 1)
                    if rout:
                        dve.wait_ge(s_ge, NE * FC * j + FC * (e + 1))
                        dve.wait_ge(s_cb, NE * j + e + 1)
                        if e >= 3:
                            dve.wait_ge(s_l2, NE * j + e - 2)
                        elif not (isinstance(i, int) and i == 1):
                            dve.wait_ge(s_l2, NE * (j - 1) + NE)
                        v.tensor_tensor(GS[:, e % 3, :, :], G[:, e % 2, :, :],
                                        PS[:, TB + e % 2, 0:N].unsqueeze(1).broadcast_to([128, FC, N]),
                                        ALU.mult).then_inc(s_sc, 1)
                if attn:
                    router_top(i)
            steps(dve, step)

        @block.tensor
        def _(pe):
            mm, tr = nc.tensor.matmul, nc.tensor.transpose

            def zero(b):
                return isinstance(b, int) and b == 0

            def tok(b):
                pe.wait_ge(s_x, 96 * (b + 1))
                if zero(b):
                    pe.wait_ge(s_wtok, 16)
                    pe.wait_ge(s_one, 1)
                elif isinstance(b, int) and b == 1:
                    pe.wait_ge(s_rope, 4 * b)
                else:
                    pe.wait_ge(s_x2Te, b - 1)
                    pe.wait_ge(s_t3, b - 2) if not (isinstance(b, int) and b == 2) else None
                xv = xt[:].rearrange("p (h w q) -> p h w q", w=HP, q=P16)
                for t in range(2):
                    for q in range(QH):
                        last = mm(PS[0:R, MA, t * D:(t + 1) * D], xv[:, t * QROWS:(t + 1) * QROWS, :, q],
                                  wtok[:, q, :], start=(q == 0), stop=(q == QH - 1))
                last.then_inc(s_tok, 1)
            QROWS = HP // 2

            def xn_T(b):
                pe.wait_ge(s_xn, b + 1)
                pe.wait_ge(s_h0, b + 1)
                if zero(b):
                    pe.wait_ge(s_small, 16 * NSMALL)
                for t in range(NT):
                    last = tr(PS[:, MA, t * R:(t + 1) * R], xn[:, t, :], idn[0:R, 0:R])
                last.then_inc(s_xnT, 1)

            def qk(b, n):
                pe.wait_ge(s_xnTe, b + 1)
                if n == 1:
                    pe.wait_ge(s_rope, 4 * b + 2)
                elif not zero(b):
                    pe.wait_ge(s_h1, b)
                else:
                    pe.wait_ge(s_wqkv, 48)
                for m, bank in ((0, MB), (1, MA)):
                    w = (2 * n + m) * D
                    mm(PS[:, bank, 0:NP], wqkv[:, w:w + D], xnT[:], start=True, stop=True).then_inc(s_qk, 1)

            def vproj(b):
                pe.wait_ge(s_rope, 4 * b + 4)
                for t in range(NT):
                    last = mm(PS[0:R, MB, t * D:(t + 1) * D], xnT[:, t * R:(t + 1) * R], wqkv[:, 4 * D:5 * D],
                              start=True, stop=True)
                last.then_inc(s_v, 1)

            def scores(i, g):
                pe.wait_ge(s_qg, NH * i + g + 1)
                if g == 0:
                    pe.wait_ge(s_qk_sb, 2 * i + 2)
                for t in range(NT):
                    n = NH * NT * i + NT * g + t
                    if g >= 1:
                        pe.wait_ge(s_exp, n - NT + 1)
                    elif not (isinstance(i, int) and i <= 1):
                        pe.wait_ge(s_ge, NE * FC * (i - 1))
                    mm(PS[0:R, t, 0:N], qg[:, g, t * R:(t + 1) * R], kT[:, 0:N], start=True,
                       stop=True).then_inc(s_lg, 1)

            def probs_T(i, g):
                pe.wait_ge(s_nrm, NH * i + g + 1)
                for t in range(NT):
                    n = NT * g + t
                    if n >= 2:
                        pe.wait_ge(s_at, NH * NT * i + n - 1)
                    elif not (isinstance(i, int) and i <= 1):
                        pe.wait_ge(s_sc, NE * (i - 1))
                    elif not zero(i):
                        pe.wait_ge(s_at, NH * NT * i)
                    for u in range(NT):
                        last = tr(PS[0:R, TB + n % 2, u * R:(u + 1) * R], E[:, g % 2, u, t * R:(t + 1) * R],
                                  idn[0:R, 0:R])
                    last.then_inc(s_tr, 1)

            def weighted(i, g):
                pe.wait_ge(s_at, NH * NT * i + NT * (g + 1))
                pe.wait_ge(s_vp, NH * i + g + 1)
                if g == 0 and not zero(i):
                    if isinstance(i, int) and i == 1:
                        pe.wait_ge(s_ot, i)
                    else:
                        pe.wait_ge(s_comb, i - 1)
                for t in range(NT):
                    last = mm(acc, VP[:, g, t, :], AT[:, g % 2, t, 0:N], start=(g == 0 and t == 0),
                              stop=(g == NH - 1 and t == NT - 1))
                last.then_inc(s_av, 1)

            def proj(i):
                pe.wait_ge(s_ot, i + 1)
                if zero(i):
                    pe.wait_ge(s_vb, 1)
                else:
                    pe.wait_ge(s_cT, i)
                for t in range(NT):
                    last = mm(PS[0:R, MB, t * D:(t + 1) * D], oT[:, t * R:(t + 1) * R], wout[:], start=True, stop=True)
                last.then_inc(s_proj, 1)

            def x2T_(i, emb):
                pe.wait_ge(s_xh, i + 1)
                if emb:
                    pe.wait_ge(s_rope, 4 * (i + 2))
                else:
                    pe.wait_ge(s_t3, i - 1)
                for t in range(NT):
                    last = tr(PS[:, MA, t * R:(t + 1) * R], xh[:, t, :], idn[0:R, 0:R])
                last.then_inc(s_x2T, 1)

            def gate(i, emb):
                pe.wait_ge(s_x2Te, i + 1)
                if emb:
                    pe.wait_ge(s_vb, i + 2)
                else:
                    pe.wait_ge(s_h1, i + 1)
                for t in range(NT):
                    last = mm(PS[0:R, MB, t * NE:(t + 1) * NE], x2T[:, t * R:(t + 1) * R], wgate[:],
                              start=True, stop=True)
                last.then_inc(s_gate, 1)

            def comb_T(k):
                pe.wait_ge(s_comb, k + 1)
                pe.wait_ge(s_x2Te, k + 2) if not (isinstance(k, int) and k + 2 > B) else None
                for t in range(NT):
                    last = tr(PS[0:R, MA, t * D:(t + 1) * D], comb[:, t * R:(t + 1) * R], idn[:, :])
                last.then_inc(s_cmT, 1)

            def conf_T(j):
                pe.wait_ge(s_chl, 3 * (j + 1))
                pe.wait_ge(s_gl, j + 1)
                for t in range(NT):
                    last = tr(PS[0:2 * NE, MB, t * R:(t + 1) * R], chl[:, t, :], idn[0:R, 0:R])
                last.then_inc(s_cTp, 1)

            def conf(j, e, attn):
                if e == 0:
                    pe.wait_ge(s_cT, j + 1)
                if e >= 2:
                    pe.wait_ge(s_sc, NE * j + e - 1)
                elif attn:
                    pe.wait_ge(s_at, NH * NT * (j + 2))
                else:
                    pe.wait_ge(s_sc, NE * j)
                mm(PS[:, TB + e % 2, 0:NV], selr[:, e, :], cT[:, 0:NV], start=True, stop=True).then_inc(s_cb, 1)

            def hidden(j, e, attn):
                for c in range(FC):
                    n = FC * e + c
                    if n >= RING:
                        pe.wait_ge(s_ge, NE * FC * j + n - RING + 1)
                    elif attn:
                        pe.wait_ge(s_exp, NH * NT * (j + 2))
                    else:
                        pe.wait_ge(s_ge, NE * FC * j)
                    if n == 0:
                        pe.wait_ge(s_xhl, j + 1)
                    w = slice(n * 128, (n + 1) * 128)
                    mm(PS[:, n % RING, 0:NV], w1hi[:, w], xhi[:, 0:NV], start=True, stop=False)
                    mm(PS[:, n % RING, 0:NV], w1hi[:, w], xlo[:, 0:NV], start=False, stop=False)
                    mm(PS[:, n % RING, 0:NV], w1lo[:, w], xhi[:, 0:NV], start=False, stop=True).then_inc(s_l1, 1)

            def second(j, e, attn):
                if e == 0:
                    if attn:
                        pe.wait_ge(s_ot, j + 2)
                    else:
                        pe.wait_ge(s_comb, j)
                    mm(PS[:, ACC, 0:NV], b2hi[:], cT[:, 0:NV], start=True, stop=False)
                    mm(PS[:, ACC, 0:NV], b2lo[:], cT[:, 0:NV], start=False, stop=False)
                pe.wait_ge(s_sc, NE * j + e + 1)
                for c in range(FC):
                    last = mm(acc, w2s[:, FC * e + c, :], GS[:, e % 3, c, :], start=False,
                              stop=(e == NE - 1 and c == FC - 1))
                last.then_inc(s_l2, 1)

            tok(0)
            xn_T(0)
            qk(0, 0)
            qk(0, 1)
            vproj(0)

            def step(i, full=False):
                attn, rout, outp, emb = parts(i, full)
                j, k = i - 1, i - 2
                for g in range(NH + 2):
                    if attn and g < NH:
                        scores(i, g)
                    if attn and g >= 2:
                        weighted(i, g - 2)
                    if attn and 1 <= g <= NH:
                        probs_T(i, g - 1)
                    if g == 1 and outp:
                        comb_T(k)
                    if g == 4 and rout:
                        conf_T(j)
                if rout and not full and i == 1:
                    pe.wait_ge(s_wr, 4)
                    pe.wait_ge(s_w2, 16)
                if emb:
                    tok(i + 1)
                for e in range(NE + 2):
                    if rout and e < NE:
                        conf(j, e, attn)
                        hidden(j, e, attn)
                    if rout and e >= 2:
                        second(j, e - 2, attn)
                    if e == 0 and attn:
                        proj(i)
                    if e == 2 and emb:
                        xn_T(i + 1)
                    if e == 3 and emb:
                        qk(i + 1, 0)
                    if e == 4 and emb:
                        qk(i + 1, 1)
                    if e == 5:
                        if emb:
                            vproj(i + 1)
                        if attn:
                            x2T_(i, emb)
                    if e == 7 and attn:
                        gate(i, emb)
            steps(pe, step)


def kernel(x, txt, L0_tok_w, L0_tok_b, L0_attn_w_qkv, L0_attn_b_qkv, L0_attn_w_pre, L0_attn_w_post, L0_attn_w_out,
           L0_attn_b_out, L0_ffn_Wg, L0_ffn_W1, L0_ffn_b1, L0_ffn_W2, L0_ffn_b2, L0_ffn_ln_g, L0_ffn_ln_b,
           L0_ffn_out_g, L0_ffn_out_b):
    import concourse.bacc as bacc
    from concourse.bass_utils import run_bass_kernel_spmd

    def a(v):
        return np.asarray(v)

    f = np.float32
    wtok = np.zeros((KR + 1, QH, D), f)
    wtok[:KR] = a(L0_tok_w).reshape(D, C, P16, 2, QH).transpose(3, 1, 2, 4, 0).reshape(KR, QH, D)
    wtok[KR, 0] = a(L0_tok_b)
    partner = np.arange(D) ^ (DH // 4)
    wq, wk, wv = a(L0_attn_w_qkv).reshape(3, D, D)
    bq, bk, bvv = a(L0_attn_b_qkv).reshape(3, D)
    wqkv = np.concatenate([wq.T, wq[partner].T, wk.T, wk[partner].T, wv.T], axis=1)
    bqk = np.stack([bq, bq[partner], bk, bk[partner]], axis=1)
    inv = (1.0 / f(10000.0) ** (np.arange(0, DH, 4, dtype=f) / f(DH))).astype(f)
    pos = np.arange(NP)
    low, chunk = (pos % 64).astype(f), (pos // 64).astype(f)
    rope = np.zeros((D, 2, NP), f)
    for p in range(D):
        d = p % DH
        ang = (low if d < DH // 2 else chunk) * inv[d % 4]
        rope[p, 0] = np.cos(ang)
        rope[p, 1] = np.sin(ang) * (1 if d & 4 else -1)
    sel = np.zeros((2 * NE, NE, 128), f)
    for e in range(NE):
        sel[e, e] = sel[NE + e, e] = 1.0

    def rows(vec):
        return np.repeat(a(vec)[None, :], R, axis=0)

    arrays = {
        "x": a(x), "txt": a(txt), "w_tok": wtok, "w_qkvr": wqkv, "b_qkr": bqk, "b_v": rows(bvv),
        "w_pre": np.repeat(a(L0_attn_w_pre).T, DH, axis=0),
        "w_post": np.repeat(np.repeat(a(L0_attn_w_post).T, DH, axis=1)[None], R, axis=0),
        "w_out": a(L0_attn_w_out).T, "b_out": rows(L0_attn_b_out), "w_gate": a(L0_ffn_Wg),
        "w1": a(L0_ffn_W1).transpose(1, 0, 2).reshape(D, NE * FH),
        "b1": a(L0_ffn_b1).reshape(NE * FC, 128).T,
        "w2": a(L0_ffn_W2).reshape(NE * FC, 128, D).transpose(1, 0, 2),
        "b2": np.concatenate([a(L0_ffn_b2)] * 2, axis=0),
        "ln_g": a(L0_ffn_ln_g)[:, None], "ln_b": a(L0_ffn_ln_b)[:, None],
        "out_g": rows(L0_ffn_out_g), "out_b": rows(L0_ffn_out_b),
        "rope": rope, "ident": np.eye(128, dtype=f), "iota": np.repeat(np.arange(NE, dtype=f)[None], R, axis=0),
        "sel": sel,
    }
    nc = bacc.Bacc("TRN2", target_bir_lowering=False, num_devices=1)
    ins, args = {}, []
    for name, v in arrays.items():
        v = np.ascontiguousarray(v)
        ins[f"in_{name}"] = v
        args.append(nc.dram_tensor(f"in_{name}", v.shape, mybir.dt.from_np(v.dtype), kind="ExternalInput").ap())
    args.append(nc.dram_tensor("out_0", (B, N, D), mybir.dt.float32, kind="ExternalOutput").ap())
    early_fusion_kernel(nc, *args)
    r = run_bass_kernel_spmd(nc, [ins], core_ids=[0])
    return r.results[0]["out_0"]
```

```python
import numpy as np
import concourse.bass as bass
from concourse import mybir
from contextlib import ExitStack

B, C, IMG, P16 = 32, 3, 224, 16
HP = IMG // P16
TXT, D, NH, DH = 77, 128, 8, 16
NE, FH = 8, 512
NPATCH = HP * HP
N = NPATCH + TXT
R = NPATCH // 2
NT = 3
NV = N + N % 2
NP = NT * R
QH = P16 // 2
KR = C * P16 * 2
FC = FH // 128
EPS = 1e-5
ROW = D + 2 * NE
REGION = B * N + 128
TILES = (2 * B * N + NE * 127) // 128
TILES += -TILES % 4
DUMMY = NE * REGION
UP = 4


def early_fusion_kernel(nc, x, txt, w_tok, w_qkvr, b_qkr, b_v, w_pre, w_post, w_out, b_out, w_gate,
                        w1, b1, w2, b2, ln_g, ln_b, out_g, out_b, rope, ident, iota, consts, tri, pick, tail,
                        tiota, routed, results, h1_dram, out):
    f32, f32r, u32, i32, bf16 = (mybir.dt.float32, mybir.dt.float32r, mybir.dt.uint32, mybir.dt.int32,
                                 mybir.dt.bfloat16)
    ALU, ACT, AX = mybir.AluOpType, mybir.ActivationFunctionType, mybir.AxisListType
    ctx = ExitStack()
    with ctx:
        def sb(name, shape, dt=f32):
            return ctx.enter_context(nc.sbuf_tensor(name, shape, dt))

        def sem(name):
            return ctx.enter_context(nc.semaphore(name))

        wtok = sb("wtok", [KR + 1, QH, D])
        wqkv = sb("wqkv", [D, 5 * D])
        bqk = sb("bqk", [D, 4])
        bv = sb("bv", [R, D])
        wpre = sb("wpre", [D, NH])
        wpost = sb("wpost", [R, NH, D])
        wout = sb("wout", [D, D])
        bout = sb("bout", [R, D])
        wgate = sb("wgate", [D, NE])
        w1hi = sb("w1hi", [D, NE * FH], f32r)
        w1lo = sb("w1lo", [D, NE * FH], f32r)
        b1hl = sb("b1hl", [2, NE * FH], f32r)
        w2s = sb("w2s", [128, NE * FC * D])
        b2hl = sb("b2hl", [2, NE * D], f32r)
        lng = sb("lng", [D, 1])
        lnb = sb("lnb", [D, 1])
        outg = sb("outg", [R, D])
        outb = sb("outb", [R, D])
        cosT = sb("cosT", [D, 2, NP])
        idn = sb("idn", [128, 128])
        iot = sb("iot", [R, NE])
        mhalf = sb("mhalf", [R, NT])
        epsT = sb("epsT", [R, NT])
        mone = sb("mone", [R, NT])
        pk = sb("pk", [2, 2])
        one2 = sb("one2", [2, 128])
        ones2 = sb("ones2", [2, 128], f32r)
        cst = sb("cst", [R, 4, NT, NE])
        trf = sb("trf", [R, 2, R])
        trb = sb("trb", [R, 2, R], bf16)
        stage = sb("stage", [128, 2, 2048])
        xt = sb("xt", [KR + 1, HP * IMG])
        H0 = sb("H0", [R, NT, D])
        HB = sb("HB", [R, 2, NT, D])
        bst = sb("bst", [R, NT, 6])
        hold = sb("hold", [R, 1])
        holdp = sb("holdp", [R, 2 + UP])
        mv1 = sb("mv1", [R, NT, 2])
        rs1 = sb("rs1", [R, NT])
        xn = sb("xn", [R, NT, D])
        xnT = sb("xnT", [D, NP])
        rc = sb("rc", [D, 2, NP])
        rsn = sb("rsn", [D, 2, NP])
        qT = sb("qT", [D, 2, NP])
        kT = sb("kT", [D, NP])
        khi = sb("khi", [D, 2, NP], f32r)
        klo = sb("klo", [D, 2, NP], f32r)
        QR = 2
        qhi = sb("qhi", [D, QR, NP], f32r)
        qlo = sb("qlo", [D, QR, NP], f32r)
        V = sb("V", [R, NT, D])
        VP = sb("VP", [R, NH, NT, D])
        nmax = sb("nmax", [R, NH * NT])
        esum = sb("esum", [R, NH * NT])
        rsum = sb("rsum", [R, NH * NT])
        E = sb("E", [R, 2, NT, NP])
        AT = sb("AT", [R, 2, NT, NP])
        oT = sb("oT", [D, NP])
        H1 = sb("H1", [R, NT, D])
        mv2 = sb("mv2", [R, NT, 2])
        nr2 = sb("nr2", [R, 2, NT])
        kept = sb("kept", [R, B, 2, NT])
        nm2 = sb("nm2", [R, NT])
        tv2 = sb("tv2", [R, 3, NT])
        rr2 = sb("rr2", [R, NT])
        y2 = sb("y2", [R, NT, D])
        xr = sb("xr", [R, 2, NT, ROW])
        x2T = sb("x2T", [D, NP])
        gl = sb("gl", [R, NT, NE])
        m8 = sb("m8", [R, NT, 8])
        ix8 = sb("ix8", [R, NT, 8], u32)
        ixf = sb("ixf", [R, 2, NT])
        dl = sb("dl", [R, NT])
        ed = sb("ed", [R, NT])
        ed1 = sb("ed1", [R, NT])
        cf = sb("cf", [R, 2, NT])
        eq = sb("eq", [R, 2, NT, NE])
        mk = sb("mk", [R, 2, NT, NE])
        cm = sb("cm", [R, 2, NT, NE])
        ms = sb("ms", [R, NT, NE])
        msb = sb("msb", [R, NT, NE], bf16)
        dd = sb("dd", [R, NT, NE])
        tokb = sb("tokb", [R, NT, NE])
        base = sb("base", [R, NE])
        ps_ = sb("pos", [R, NT, NE])
        sl = sb("sl", [R, 2, NT, NE])
        slf = sb("slf", [R, 2, NT])
        slu = sb("slu", [R, 2, 2, NT], u32)
        cnt = sb("cnt", [1, NE])
        cni = sb("cni", [1, 2, NE], i32)
        ntl = sb("ntl", [1, NE])
        cum = sb("cum", [1, NE])
        adr = sb("adr", [1, 3, NE])
        cmp_, cda = (stage[0:1, i, 0:TILES * NE].rearrange("p (n e) -> p n e", e=NE) for i in range(2))
        tio = sb("tio", [1, 2, TILES])
        tabf = sb("tabf", [1, 4, TILES])
        tab = sb("tab", [1, 2, TILES], u32)
        basu = sb("basu", [1, NE], u32)
        tailt = sb("tailt", [128, ROW])
        XB = sb("XB", [128, UP, ROW])
        xa = sb("xa", [128, 2, D])
        xhi = sb("xhi", [128, 2, D], f32r)
        xlo = sb("xlo", [128, 2, D], f32r)
        hs = sb("hs", [128, 2, FH])
        GT = sb("GT", [128, 2, FH])
        cd = sb("cd", [128, UP, 2])
        du = sb("du", [128, UP, 1], u32)
        OT = sb("OT", [128, UP, D])
        w = NT * D

        def parts(buf, count, size, at=0):
            flat = buf[:, at:at + count * size]
            return [flat[:, i * size:(i + 1) * size].rearrange("p (t d) -> p t d", t=NT) for i in range(count)]
        flat_vp = VP[:].rearrange("p h t d -> p (h t d)")
        RES = [a.rearrange("p t (k d) -> p t k d", k=2)
               for a in parts(stage[0:R].rearrange("p a n -> p (a n)"), UP, 2 * w)]
        H3, T3 = parts(flat_vp, UP, w), parts(flat_vp, UP, w, UP * w)
        Y3 = parts(E[:].rearrange("p a t n -> p (a t n)"), UP, w)
        fin = parts(AT[:].rearrange("p a t n -> p (a t n)"), UP, w)
        nr3 = sb("nr3", [R, UP, 2, NT])
        mv3 = sb("mv3", [R, UP, NT, 2])
        rs3 = sb("rs3", [R, UP, NT])

        PS = ctx.enter_context(nc.psum_tensor("PS", [128, 8, 512], f32))
        TB, ACC, MA, MB = 3, 5, 6, 7
        acc = PS[:, ACC, 0:N]

        SMALL = ((bv, b_v), (wpre, w_pre), (wpost, w_post), (wout, w_out), (bout, b_out), (wgate, w_gate),
                 (lng, ln_g), (lnb, ln_b), (outg, out_g), (outb, out_b), (idn, ident), (iot, iota),
                 (cst, consts), (trf, tri))
        NSMALL = len(SMALL)

        names = """tok_weights qkv_weights small_weights w1_loaded w2_loaded b1_loaded setup_gpsimd setup_vector
            weights_rounded bias_steps x_loaded txt_loaded kept_h norm_kept tok_ps xnT_ps qk_ps v_ps h0 bn1 bn2 bn3
            stats1 stats2 stats3 rstd1 rstd1_steps xn xnT_sb hb rope qk_sb k_hi k_lo q_hi q_lo vb vp scores_ps
            max exp recip probs probsT_ps probsT_sb av_ps attn_sb proj_ps h1 rstd2 rstd2_steps y2 xhat x2T_ps
            x2T_sb gate_ps gate_sb top8 logit_gap gap_exp conf_steps masks routed_cols rank_ps pos_steps pos_read
            slots scat0 scat1 table_steps table_ready tails row0 row1 row2 row3 xT_ps xa x_hi x_lo hidden_ps
            gelu hT_ps hT_sb out_ps out_sb cols place out0 out1 out2 out3 in0 in1 in2 in3 nr3 y3 t3
            rstd3 rstd3_steps carried residual3 c3 fin st0 st1 st2 st3"""
        S = {n: sem(n) for n in names.split()}

        block = ctx.enter_context(nc.Block())

        def below(b, n):
            return isinstance(b, int) and b < n

        def steps(eng, step):
            def peeled(i):
                step(i, i % 2, dict(attn=i < B, emb=i < B - 1, res=1 <= i <= B, rout=i >= 2, late=i >= 3,
                                     load=i < B - 2))
            every = dict(attn=True, emb=True, res=True, rout=True, late=True, load=True)
            for i in range(4):
                peeled(i)
            with eng.Fori(4, B - 3, 2) as i:
                step(i, 0, every)
                step(i + 1, 1, every)
            for i in range(B - 2, B + 2):
                peeled(i)

        def slots(eng, total, stages, by_expert=()):
            ahead = [a for a, _ in stages]

            def expert(t):
                return eng.value_load(tab[0:1, 0, bass.ds(t, 1)], min_val=0, max_val=NE - 1)

            def peeled(s):
                for a, stage_ in stages:
                    if 0 <= s + a < total:
                        stage_(s + a, (s + a) % UP, *([expert(s + a)] if stage_ in by_expert else []))
            for s in range(-max(ahead), 2 * UP):
                peeled(s)
            with eng.Fori(2 * UP, total - 2 * UP + 1, UP) as s:
                offsets = sorted({u + a for a, stage_ in stages if stage_ in by_expert for u in range(UP)})
                loaded = {n: expert(s + n) for n in offsets}
                for u in range(UP):
                    for a, stage_ in stages:
                        stage_(s + (u + a), (u + a) % UP, *([loaded[u + a]] if stage_ in by_expert else []))
            for s in range(total - UP, total - min(ahead)):
                peeled(s)

        @block.sync
        def _(sp):
            sp.dma_start(wtok[:], w_tok).then_inc(S["tok_weights"], 16)

            def load(b):
                if not below(b, 1):
                    sp.wait_ge(S["tok_ps"], b)
                for half in range(2):
                    for c in range(C):
                        r0 = half * C * P16 + c * P16
                        dst = xt[r0:r0 + P16, :].rearrange("p (h w) -> p h w", w=IMG)[:, :, 0:IMG - QH * half]
                        src = x[b, c].rearrange("(h p) w -> p h w", p=P16)[:, :, QH * half:IMG]
                        sp.dma_start(dst, src).then_inc(S["x_loaded"], 16)

            def load_txt(b):
                if below(b, 1):
                    sp.wait_ge(S["setup_gpsimd"], 1)
                else:
                    sp.wait_ge(S["xn"], b)
                    sp.wait_ge(S["hb"], b)
                sp.dma_start(H0[0:TXT, 2, :], txt[b]).then_inc(S["txt_loaded"], 16)

            load(0)
            load_txt(0)
            sp.dma_start(wqkv[:], w_qkvr).then_inc(S["qkv_weights"], 16)
            sp.dma_start(cosT[:], rope).then_inc(S["qkv_weights"], 16)
            sp.dma_start(bqk[:], b_qkr).then_inc(S["qkv_weights"], 16)
            for dst, src in SMALL:
                sp.dma_start(dst[:], src).then_inc(S["small_weights"], 16)
            load(1)
            load_txt(1)

            def step(i, par, has):
                if has["load"]:
                    load(i + 2)
                if has["res"]:
                    sp.wait_ge(S["h1"], i)
                    sp.dma_start(h1_dram[i - 1], H1[:].rearrange("p t d -> p (t d)")).then_inc(S["kept_h"], 16)
                if has["load"]:
                    load_txt(i + 2)
            steps(sp, step)

            sp.wait_ge(S["w2_loaded"], 64)
            sp.wait_ge(S["table_ready"], 1)
            for e in range(NE):
                row = sp.value_load(basu[0:1, e:e + 1], min_val=0, max_val=DUMMY - 128)
                sp.dma_start(routed[bass.ds(row, 128), :], tailt[:]).then_inc(S["tails"], 16)
            sp.dma_start(routed[DUMMY:DUMMY + 128, :], tailt[:]).then_inc(S["tails"], 16)
            sp.wait_ge(S["tails"], 16 * (NE + 1))
            sp.wait_ge(S["scat0"], 48 * B)
            sp.wait_ge(S["scat1"], 48 * B)

            def load_tile(t, u):
                row = sp.value_load(tab[0:1, 1, bass.ds(t, 1)], min_val=0, max_val=DUMMY)
                if not below(t, UP):
                    sp.wait_ge(S["xT_ps"], t - UP + 1)
                    sp.wait_ge(S["cols"], t - UP + 1)
                sp.dma_start(XB[:, u, :], routed[bass.ds(row, 128), :]).then_inc(S[f"row{u}"], 16)
            slots(sp, TILES, [(0, load_tile)])

            for u in range(UP):
                sp.wait_ge(S[f"out{u}"], 16 * (TILES // UP))
            sp.wait_ge(S["kept_h"], 16 * B)

            def load_image(k, p):
                if not below(k, UP):
                    sp.wait_ge(S["fin"], k - UP + 1)
                rows = results[bass.ds(k * N, N), :]
                for t in range(NT):
                    n = R if t < 2 else TXT
                    sp.dma_start(RES[p][0:n, t], rows[t * R:t * R + n, :].rearrange("p (k d) -> p k d", k=2)
                                 ).then_inc(S[f"in{p}"], 16)
                sp.dma_start(H3[p], h1_dram[k].rearrange("p (t d) -> p t d", t=NT)).then_inc(S[f"in{p}"], 16)

            def store(k, p):
                sp.wait_ge(S["fin"], k + 1)
                for t in range(NT):
                    n = R if t < 2 else TXT
                    sp.dma_start(out[k, t * R:t * R + n, :], fin[p][0:n, t, :]).then_inc(S[f"st{p}"], 16)
            slots(sp, B, [(3, load_image), (0, store)])
            for u in range(UP):
                sp.wait_ge(S[f"st{u}"], 12 * B)

        @block.gpsimd
        def _(pool):
            g_ = nc.gpsimd
            g_.memset(H0[:], 0.0).then_inc(S["setup_gpsimd"], 1)
            g_.memset(E[:], 0.0).then_inc(S["setup_gpsimd"], 1)
            g_.memset(oT[:], 0.0).then_inc(S["setup_gpsimd"], 1)
            g_.memset(mhalf[:], -0.5)
            g_.memset(mone[:], -1.0)
            g_.memset(epsT[:], EPS).then_inc(S["setup_gpsimd"], 1)
            pool.wait_ge(S["small_weights"], 16 * NSMALL)
            pool.wait_ge(S["setup_gpsimd"], 4)
            g_.tensor_scalar(wpre[:], wpre[:], DH ** -0.5, None, ALU.mult).then_inc(S["setup_gpsimd"], 1)

            def carry_wait(c):
                return g_.tensor_tensor(holdp[:, c:c + 1], epsT[:, 0:1], epsT[:, 0:1], ALU.add)

            def norm1(b):
                pool.wait_ge(S["stats1"], b + 1)
                g_.tensor_tensor(rs1[:], mv1[:, :, 1], epsT[:], ALU.add).then_inc(S["rstd1_steps"], 1)
                pool.wait_ge(S["rstd1_steps"], b + 1)
                g_.tensor_tensor(rs1[:], rs1[:], mhalf[:], ALU.pow).then_inc(S["rstd1"], 1)

            def hb(b, par):
                pool.wait_ge(S["h0"], b + 1)
                pool.wait_ge(S["txt_loaded"], 16 * (b + 1))
                if not below(b, 2):
                    pool.wait_ge(S["h1"], b - 1)
                g_.tensor_tensor(HB[:, par], H0[:], bout[:].unsqueeze(1).broadcast_to([R, NT, D]),
                                 ALU.add).then_inc(S["hb"], 1)

            def rope_add(b, par, n):
                pool.wait_ge(S["rope"], 4 * b + 2 * n + 2)
                if n == 0:
                    if not below(b, 2):
                        pool.wait_ge(S["q_lo"], NH * (b - 1))
                    dst = qT[:, par]
                else:
                    if not below(b, 1):
                        pool.wait_ge(S["k_hi"], b)
                        pool.wait_ge(S["k_lo"], b)
                    dst = kT[:]
                g_.tensor_tensor(dst, rc[:, n, :], rsn[:, n, :], ALU.add).then_inc(S["qk_sb"], 1)

            def vpost(b):
                pool.wait_ge(S["vb"], b + 1)
                for h in range(NH):
                    if not below(b, 1):
                        pool.wait_ge(S["av_ps"], NH * (b - 1) + h + 1)
                    g_.tensor_tensor(VP[:, h], V[:], wpost[:, h, :].unsqueeze(1).broadcast_to([R, NT, D]),
                                     ALU.mult).then_inc(S["vp"], 1)

            def norm2(b):
                st = S["rstd2_steps"]
                pool.wait_ge(S["stats2"], b + 1)
                g_.tensor_tensor(tv2[:, 0], mv2[:, :, 1], epsT[:], ALU.add).then_inc(st, 1)
                pool.wait_ge(st, 6 * b + 1)
                g_.tensor_tensor(nr2[:, 0], tv2[:, 0], mhalf[:], ALU.pow).then_inc(st, 1)
                pool.wait_ge(st, 6 * b + 2)
                g_.tensor_tensor(nm2[:], mv2[:, :, 0], nr2[:, 0], ALU.mult)
                g_.tensor_tensor(tv2[:, 1], mv2[:, :, 1], nr2[:, 0], ALU.mult).then_inc(st, 1)
                pool.wait_ge(st, 6 * b + 3)
                g_.tensor_tensor(nr2[:, 1], nm2[:], mone[:], ALU.mult).then_inc(S["rstd2"], 1)
                g_.tensor_tensor(tv2[:, 2], tv2[:, 1], nr2[:, 0], ALU.mult).then_inc(st, 1)
                pool.wait_ge(st, 6 * b + 4)
                g_.tensor_tensor(tv2[:, 0], tv2[:, 2], epsT[:], ALU.add).then_inc(st, 1)
                pool.wait_ge(st, 6 * b + 5)
                g_.tensor_tensor(rr2[:], tv2[:, 0], mhalf[:], ALU.pow).then_inc(st, 1)

            def scatter(j, par):
                pool.wait_ge(S["slots"], j + 1)
                pool.wait_ge(S["xhat"], j + 1)
                carry_wait(par)
                for k in range(2):
                    for t in range(NT):
                        rows = R if t < 2 else TXT
                        g_.indirect_dma_start(
                            out=routed, out_offset=bass.IndirectOffsetOnAxis(ap=slu[0:rows, par, k, t:t + 1], axis=0),
                            in_=xr[0:rows, par, t, :], in_offset=None).then_inc(S[f"scat{par}"], 16)

            norm1(0)
            hb(0, 0)
            rope_add(0, 0, 0)
            rope_add(0, 0, 1)
            vpost(0)

            def step(i, par, has):
                if has["emb"]:
                    norm1(i + 1)
                if has["late"]:
                    scatter(i - 3, 1 - par)
                if has["res"]:
                    norm2(i - 1)
                if has["emb"]:
                    rope_add(i + 1, 1 - par, 0)
                    rope_add(i + 1, 1 - par, 1)
                    hb(i + 1, 1 - par)
                    vpost(i + 1)
            steps(pool, step)
            scatter(B - 1, 1)

            def scatter_out(t, u):
                if not below(t, UP):
                    pool.wait_ge(S["carried"], t - UP + 1)
                pool.wait_ge(S["out_sb"], t + 1)
                pool.wait_ge(S["place"], t + 1)
                carry_wait(2 + u).then_inc(S["carried"], 1)
                g_.indirect_dma_start(
                    out=results.rearrange("n (k d) -> (n k) d", k=2),
                    out_offset=bass.IndirectOffsetOnAxis(ap=du[:, u, :], axis=0), in_=OT[:, u, :], in_offset=None,
                    bounds_check=2 * B * N - 1, oob_is_err=False).then_inc(S[f"out{u}"], 16)
            slots(pool, TILES, [(0, scatter_out)])

            def residual3(k, p):
                pool.wait_ge(S["y3"], k + 1)
                g_.tensor_tensor(H3[p], H3[p], outb[:].unsqueeze(1).broadcast_to([R, NT, D]), ALU.add
                                 ).then_inc(S["residual3"], 1)

            def norm3(k, p):
                pool.wait_ge(S["stats3"], k + 1)
                g_.tensor_tensor(rs3[:, p], mv3[:, p, :, 1], epsT[:], ALU.add).then_inc(S["rstd3_steps"], 1)
                pool.wait_ge(S["rstd3_steps"], k + 1)
                g_.tensor_tensor(rs3[:, p], rs3[:, p], mhalf[:], ALU.pow).then_inc(S["rstd3"], 1)
            slots(pool, B, [(1, residual3), (0, norm3)])

        @block.scalar
        def _(act):
            for a in range(2):
                act.dma_start(stage[:, a, :], w1[:, a * 2048:(a + 1) * 2048]).then_inc(S["w1_loaded"], 16)
            for dst, src in ((w2s, w2), (pk, pick), (tio, tiota), (tailt, tail)):
                act.dma_start(dst[:], src).then_inc(S["w2_loaded"], 16)
            act.wait_ge(S["weights_rounded"], 2)
            for a in range(2):
                act.dma_start(stage[0:2, a, :], b1[:, a * 2048:(a + 1) * 2048]).then_inc(S["b1_loaded"], 16)
            act.wait_ge(S["bias_steps"], 8)
            act.dma_start(stage[0:2, 0, 0:NE * D], b2).then_inc(S["b1_loaded"], 16)

            def q_hi(i, par, g):
                act.wait_ge(S["qk_sb"], 2 * i + 1)
                if below(i, 1) and g == 0:
                    act.wait_ge(S["setup_gpsimd"], 5)
                if not (below(i, 1) and g < QR):
                    act.wait_ge(S["scores_ps"], NT * (NH * i + g - QR + 1))
                nc.scalar.activation(qhi[:, g % QR, :], qT[:, par, :], ACT.Copy, scale=wpre[:, g:g + 1]
                                     ).then_inc(S["q_hi"], 1)

            def probs(i, g):
                for t in range(NT):
                    n = NT * g + t
                    act.wait_ge(S["max"], NH * NT * i + n + 1)
                    if t == 0:
                        if below(i, 1) and g < 2:
                            act.wait_ge(S["setup_gpsimd"], 4)
                        else:
                            act.wait_ge(S["probsT_ps"], NT * (NH * i + g - 1))
                    nc.scalar.activation(E[:, g % 2, t, 0:N], PS[0:R, t, 0:N], ACT.Exp, bias=nmax[:, n:n + 1],
                                         accum_out=esum[:, n:n + 1]).then_inc(S["exp"], 1)

            def probsT(i, g):
                for t in range(NT):
                    n = NT * g + t
                    act.wait_ge(S["probsT_ps"], NH * NT * i + n + 1)
                    if t == 0 and not (below(i, 1) and g < 2):
                        act.wait_ge(S["av_ps"], NH * i + g - 1)
                    nc.scalar.copy(AT[:, g % 2, t, :], PS[0:R, TB + n % 2, 0:NP]).then_inc(S["probsT_sb"], 1)

            def attn_out(i):
                act.wait_ge(S["av_ps"], NH * (i + 1))
                if below(i, 1):
                    act.wait_ge(S["setup_gpsimd"], 4)
                else:
                    act.wait_ge(S["proj_ps"], i)
                nc.scalar.copy(oT[:, 0:N], acc).then_inc(S["attn_sb"], 1)

            def k_hi(b, par):
                act.wait_ge(S["qk_sb"], 2 * b + 2)
                if not below(b, 2):
                    act.wait_ge(S["scores_ps"], NH * NT * (b - 1))
                nc.scalar.copy(khi[:, par], kT[:]).then_inc(S["k_hi"], 1)

            def normed2(j):
                act.wait_ge(S["rstd2"], j + 1)
                if not below(j, 1):
                    act.wait_ge(S["xhat"], j)
                for t in range(NT):
                    last = nc.scalar.activation(y2[:, t, :], H1[:, t, :], ACT.Identity, bias=nr2[:, 1, t:t + 1],
                                                scale=nr2[:, 0, t:t + 1])
                last.then_inc(S["y2"], 1)

            def xhat(j, par):
                act.wait_ge(S["y2"], j + 1)
                act.wait_ge(S["rstd2_steps"], 6 * j + 6)
                if not below(j, 2):
                    act.wait_ge(S[f"scat{par}"], 48 * (j - par))
                for t in range(NT):
                    last = nc.scalar.activation(xr[:, par, t, 0:D], y2[:, t, :], ACT.Copy, scale=rr2[:, t:t + 1])
                last.then_inc(S["xhat"], 1)

            k_hi(0, 0)
            q_hi(0, 0, 0)
            q_hi(0, 0, 1)

            def step(i, par, has):
                for g in range(NH):
                    if g == 2 and has["res"]:
                        attn_out(i - 1)
                    if has["attn"]:
                        probs(i, g)
                    if g > 0 and has["attn"]:
                        probsT(i, g - 1)
                    if g == 0 and has["res"]:
                        probsT(i - 1, NH - 1)
                    if g < NH - 2 and has["attn"]:
                        q_hi(i, par, g + 2)
                    if g >= NH - 2 and has["emb"]:
                        q_hi(i + 1, 1 - par, g + 2 - NH)
                    if g == 3 and has["rout"]:
                        act.wait_ge(S["logit_gap"], i - 1)
                        nc.scalar.activation(ed[:], dl[:], ACT.Exp).then_inc(S["gap_exp"], 1)
                    if g == 5 and has["res"]:
                        normed2(i - 1)
                    if g == 6 and has["emb"]:
                        k_hi(i + 1, 1 - par)
                    if g == 7 and has["res"]:
                        xhat(i - 1, 1 - par)
            steps(act, step)

            def affine(t, u):
                act.wait_ge(S["xT_ps"], t + 1)
                if not below(t, 2):
                    act.wait_ge(S["x_lo"], t - 1)
                nc.scalar.activation(xa[:, u % 2], PS[:, u % 2, 0:D], ACT.Identity, bias=lnb[:, 0:1],
                                     scale=lng[:, 0:1]).then_inc(S["xa"], 1)

            def gelu(t, u):
                act.wait_ge(S["hidden_ps"], t + 1)
                if not below(t, 2):
                    act.wait_ge(S["hT_ps"], t - 1)
                nc.scalar.activation(hs[:, u % 2], PS[:, 2 + u % 2, :], ACT.Gelu_apprx_tanh).then_inc(S["gelu"], 1)

            def result(t, u):
                act.wait_ge(S["out_ps"], t + 1)
                act.wait_ge(S["cols"], t + 1)
                if not below(t, UP):
                    act.wait_ge(S[f"out{u}"], 4 * (t - u))
                nc.scalar.activation(OT[:, u], PS[:, 6 + u % 2, 0:D], ACT.Copy, scale=cd[:, u, 0:1]
                                     ).then_inc(S["out_sb"], 1)
            slots(act, TILES, [(2, affine), (1, gelu), (-1, result)])

            def normed3(k, p):
                act.wait_ge(S["nr3"], k + 1)
                act.wait_ge(S[f"in{p}"], 16 * (k - p) + 64)
                if not below(k, UP):
                    act.wait_ge(S["t3"], 2 * (k - UP + 1))
                for t in range(NT):
                    last = nc.scalar.activation(Y3[p][:, t], H3[p][:, t], ACT.Identity, bias=nr3[:, p, 1, t:t + 1],
                                                scale=nr3[:, p, 0, t:t + 1])
                last.then_inc(S["y3"], 1)
            slots(act, B, [(0, normed3)])

        @block.vector
        def _(dve):
            v = nc.vector
            v.memset(xt[KR:KR + 1, :], 1.0).then_inc(S["setup_vector"], 1)
            v.memset(one2[:], 1.0).then_inc(S["setup_vector"], 1)
            dve.wait_ge(S["w1_loaded"], 32)
            for a in range(2):
                v.tensor_copy(w1hi[:, a * 2048:(a + 1) * 2048], stage[:, a, :])
            dve.wait_ge(S["setup_vector"], 2)
            v.tensor_copy(ones2[:], one2[:]).then_inc(S["setup_vector"], 1)
            dve.wait_ge(S["setup_vector"], 3)
            for a in range(2):
                v.tensor_tensor(w1lo[:, a * 2048:(a + 1) * 2048], stage[:, a, :],
                                w1hi[:, a * 2048:(a + 1) * 2048].bitcast(f32),
                                ALU.subtract).then_inc(S["weights_rounded"], 1)
            dve.wait_ge(S["w2_loaded"], 64)
            tmp = VP[0:2].rearrange("p h t d -> p (h t d)")
            bs = S["bias_steps"]
            for n, (dst, src, loaded) in enumerate(((b1hl[:, 0:2048], stage[0:2, 0], 32),
                                                    (b1hl[:, 2048:4096], stage[0:2, 1], 32),
                                                    (b2hl[:], stage[0:2, 0, 0:NE * D], 48))):
                cols = dst.shape[1]
                dve.wait_ge(S["b1_loaded"], loaded)
                v.tensor_copy(dst, src).then_inc(bs, 1)
                dve.wait_ge(bs, 4 * n + 1)
                v.tensor_tensor(tmp[:, 0:cols], src, dst.bitcast(f32), ALU.subtract).then_inc(bs, 1)
                dve.wait_ge(bs, 4 * n + 2)
                v.tensor_scalar(src, dst.bitcast(f32), pk[:, 0:1], None, ALU.mult).then_inc(bs, 1)
                dve.wait_ge(bs, 4 * n + 3)
                v.scalar_tensor_tensor(dst, tmp[:, 0:cols], pk[:, 1:2], src, ALU.mult, ALU.add).then_inc(bs, 1)
            dve.wait_ge(S["small_weights"], 16 * NSMALL)
            v.tensor_copy(trb[:], trf[:])
            v.tensor_copy(base[:], cst[:, 2, 0, :])
            v.tensor_copy(tokb[:], cst[:, 3]).then_inc(S["setup_vector"], 1)

            def stats(src, mv, b, bn, done):
                for t in range(NT):
                    last = v.bn_stats(bst[:, t, :], src[:, t, :])
                last.then_inc(bn, 1)
                dve.wait_ge(bn, b + 1)
                v.tensor_copy(hold[:], bst[:, 0, 0:1])
                for t in range(NT):
                    last = v.bn_aggr(mv[:, t, :], bst[:, t, :])
                last.then_inc(done, 1)

            def tokens(b):
                dve.wait_ge(S["tok_ps"], b + 1)
                if below(b, 1):
                    dve.wait_ge(S["setup_gpsimd"], 4)
                else:
                    dve.wait_ge(S["hb"], b)
                v.tensor_copy(H0[:, 0:2, :], PS[0:R, MA, 0:2 * D].rearrange("p (t d) -> p t d", t=2)
                              ).then_inc(S["h0"], 1)
                dve.wait_ge(S["txt_loaded"], 16 * (b + 1))
                dve.wait_ge(S["h0"], b + 1)
                stats(H0, mv1, b, S["bn1"], S["stats1"])

            def normed(b):
                dve.wait_ge(S["rstd1"], b + 1)
                if not below(b, 1):
                    dve.wait_ge(S["xnT_ps"], b)
                for t in range(NT):
                    last = v.tensor_scalar(xn[:, t, :], H0[:, t, :], mv1[:, t, 0:1], rs1[:, t:t + 1],
                                           ALU.subtract, ALU.mult)
                last.then_inc(S["xn"], 1)

            def normedT(b):
                dve.wait_ge(S["xnT_ps"], b + 1)
                if not below(b, 1):
                    dve.wait_ge(S["v_ps"], b)
                v.tensor_copy(xnT[:], PS[:, MA, 0:NP]).then_inc(S["xnT_sb"], 1)

            def rope_mul(b, n):
                for m, (dst, bank) in enumerate(((rc, MA), (rsn, MB))):
                    dve.wait_ge(S["qk_ps"], 4 * b + 2 * n + m + 1)
                    if m == 0 and not below(b, 1):
                        dve.wait_ge(S["qk_sb"], 2 * b - 1 + n)
                    v.scalar_tensor_tensor(dst[:, n, :], PS[:, bank, 0:NP], bqk[:, 2 * n + m:2 * n + m + 1],
                                           cosT[:, m, :], ALU.add, ALU.mult).then_inc(S["rope"], 1)

            def values(b):
                dve.wait_ge(S["v_ps"], b + 1)
                if not below(b, 1):
                    dve.wait_ge(S["vp"], NH * b)
                v.tensor_tensor(V[:], PS[0:R, MA, 0:NT * D].rearrange("p (t d) -> p t d", t=NT),
                                bv[:].unsqueeze(1).broadcast_to([R, NT, D]), ALU.add).then_inc(S["vb"], 1)

            def q_lo(i, par, g):
                dve.wait_ge(S["q_hi"], NH * i + g + 1)
                dve.wait_ge(S["qk_sb"], 2 * i + 1)
                v.scalar_tensor_tensor(qlo[:, g % QR, :], qT[:, par, :], wpre[:, g:g + 1],
                                       qhi[:, g % QR, :].bitcast(f32), ALU.mult, ALU.subtract).then_inc(S["q_lo"], 1)

            def k_lo(b, par):
                dve.wait_ge(S["k_hi"], b + 1)
                v.tensor_tensor(klo[:, par], kT[:], khi[:, par].bitcast(f32), ALU.subtract).then_inc(S["k_lo"], 1)

            def head_probs(i, g):
                dve.wait_ge(S["exp"], NT * (NH * i + g + 1))
                v.reciprocal(rsum[:, NT * g:NT * g + NT], esum[:, NT * g:NT * g + NT]).then_inc(S["recip"], 1)
                dve.wait_ge(S["recip"], NH * i + g + 1)
                for t in range(NT):
                    last = v.tensor_scalar(E[:, g % 2, t, 0:N], E[:, g % 2, t, 0:N],
                                           rsum[:, NT * g + t:NT * g + t + 1], None, ALU.mult)
                last.then_inc(S["probs"], 1)

            def head_max(i, g):
                for t in range(NT):
                    n = NT * g + t
                    dve.wait_ge(S["scores_ps"], NH * NT * i + n + 1)
                    v.tensor_reduce(nmax[:, n:n + 1], PS[0:R, t, 0:N], AX.X, ALU.max, negate=True
                                    ).then_inc(S["max"], 1)

            def residual(j, par):
                dve.wait_ge(S["proj_ps"], j + 1)
                dve.wait_ge(S["hb"], j + 1)
                if not below(j, 1):
                    dve.wait_ge(S["y2"], j)
                    dve.wait_ge(S["kept_h"], 16 * j)
                v.tensor_tensor(H1[:], PS[0:R, MB, 0:NT * D].rearrange("p (t d) -> p t d", t=NT), HB[:, par],
                                ALU.add).then_inc(S["h1"], 1)
                dve.wait_ge(S["h1"], j + 1)
                stats(H1, mv2, j, S["bn2"], S["stats2"])

            def keep(j):
                dve.wait_ge(S["rstd2"], j + 1)
                v.tensor_copy(kept[:, bass.ds(j, 1)].rearrange("p a n t -> p (a n) t"), nr2[:]
                              ).then_inc(S["norm_kept"], 1)

            def x2_T(j):
                dve.wait_ge(S["x2T_ps"], j + 1)
                if not below(j, 1):
                    dve.wait_ge(S["gate_ps"], j)
                v.tensor_scalar(x2T[:], PS[:, MB, 0:NP], lng[:], lnb[:], ALU.mult, ALU.add).then_inc(S["x2T_sb"], 1)

            def top(j):
                dve.wait_ge(S["gate_ps"], j + 1)
                v.tensor_copy(gl[:], PS[0:R, MB, 0:NT * NE].rearrange("p (t e) -> p t e", t=NT)
                              ).then_inc(S["gate_sb"], 1)
                dve.wait_ge(S["gate_sb"], j + 1)
                v.tensor_copy(hold[:], gl[:, 0, 0:1])
                for t in range(NT):
                    last = v.max(m8[:, t, :], gl[:, t, :])
                last.then_inc(S["top8"], 1)
                dve.wait_ge(S["top8"], j + 1)
                v.tensor_tensor(dl[:], m8[:, :, 1], m8[:, :, 0], ALU.subtract).then_inc(S["logit_gap"], 1)
                for t in range(NT):
                    last = v.max_index(ix8[:, t, :], m8[:, t, :], gl[:, t, :])
                last.then_inc(S["conf_steps"], 1)

            def experts(j):
                cs = S["conf_steps"]
                c0 = 6 * j
                dve.wait_ge(S["gap_exp"], j + 1)
                dve.wait_ge(cs, c0 + 1)
                v.tensor_scalar(ed1[:], ed[:], 1.0, None, ALU.add)
                v.tensor_copy(ixf[:].rearrange("p k t -> p t k"), ix8[:, :, 0:2]).then_inc(cs, 1)
                dve.wait_ge(cs, c0 + 2)
                v.reciprocal(cf[:, 0, :], ed1[:])
                v.tensor_tensor(eq[:].rearrange("p k t e -> p (k t) e"),
                                iot[:].unsqueeze(1).broadcast_to([R, 2 * NT, NE]),
                                ixf[:].rearrange("p k t -> p (k t)").unsqueeze(2).broadcast_to([R, 2 * NT, NE]),
                                ALU.is_equal).then_inc(cs, 1)
                dve.wait_ge(cs, c0 + 3)
                v.tensor_tensor(cf[:, 1, :], ed[:], cf[:, 0, :], ALU.mult)
                v.tensor_tensor(mk[:], eq[:], cst[:, 0:2], ALU.mult).then_inc(cs, 1)
                dve.wait_ge(cs, c0 + 4)
                v.tensor_tensor(cm[:].rearrange("p k t e -> p (k t) e"), mk[:].rearrange("p k t e -> p (k t) e"),
                                cf[:].rearrange("p k t -> p (k t)").unsqueeze(2).broadcast_to([R, 2 * NT, NE]),
                                ALU.mult)
                v.tensor_tensor(msb[:], mk[:, 0], mk[:, 1], ALU.add).then_inc(S["masks"], 1)
                v.tensor_tensor(ms[:], mk[:, 0], mk[:, 1], ALU.add).then_inc(cs, 1)

            def weights(j, par):
                cs = S["conf_steps"]
                c0 = 6 * j
                dve.wait_ge(cs, c0 + 5)
                dve.wait_ge(S["xhat"], j + 1)
                v.tensor_tensor(xr[:, par, :, D:D + NE], cm[:, 0], cm[:, 1], ALU.add)
                v.tensor_tensor(dd[:], ms[:], tokb[:], ALU.mult).then_inc(cs, 1)
                dve.wait_ge(cs, c0 + 6)
                v.tensor_tensor(xr[:, par, :, D + NE:ROW], dd[:], mk[:, 1], ALU.add)
                v.tensor_scalar(tokb[:], tokb[:], 2.0 * N, None, ALU.add).then_inc(S["routed_cols"], 1)

            def places(j, par):
                st = S["pos_steps"]
                dve.wait_ge(S["rank_ps"], j + 1)
                dve.wait_ge(S["routed_cols"], j + 1)
                v.tensor_tensor(ps_[:], PS[0:R, MB, 0:NT * NE].rearrange("p (t e) -> p t e", t=NT),
                                base[:].unsqueeze(1).broadcast_to([R, NT, NE]), ALU.add).then_inc(st, 1)
                dve.wait_ge(st, 3 * j + 1)
                for k in range(2):
                    v.tensor_tensor(sl[:, k], mk[:, k], ps_[:], ALU.mult)
                v.tensor_tensor(base[:], PS[0:R, MB, NT * NE:(NT + 1) * NE], base[:], ALU.add
                                ).then_inc(S["pos_read"], 1)
                dve.wait_ge(S["pos_read"], j + 1)
                v.tensor_reduce(slf[:], sl[:], AX.X, ALU.add).then_inc(st, 1)
                dve.wait_ge(st, 3 * j + 2)
                v.tensor_copy(slu[:, par], slf[:]).then_inc(st, 1)
                dve.wait_ge(st, 3 * j + 3)
                v.tensor_copy(hold[:], slf[:, 0, 0:1]).then_inc(S["slots"], 1)

            tokens(0)
            normed(0)
            normedT(0)
            rope_mul(0, 0)
            rope_mul(0, 1)
            values(0)
            k_lo(0, 0)
            q_lo(0, 0, 0)

            def step(i, par, has):
                for g in range(NH):
                    if g > 0 and has["attn"]:
                        head_probs(i, g - 1)
                    if g == 0 and has["res"]:
                        head_probs(i - 1, NH - 1)
                    if has["attn"]:
                        head_max(i, g)
                        if g < NH - 1:
                            q_lo(i, par, g + 1)
                    if g == 0 and has["rout"]:
                        x2_T(i - 2)
                        keep(i - 2)
                    if g == 1 and has["emb"]:
                        tokens(i + 1)
                    if g == 2:
                        if has["emb"]:
                            normed(i + 1)
                        if has["rout"]:
                            top(i - 2)
                    if g == 3:
                        if has["res"]:
                            residual(i - 1, 1 - par)
                        if has["emb"]:
                            normedT(i + 1)
                    if g in (4, 5) and has["emb"]:
                        rope_mul(i + 1, g - 4)
                    if g == 4 and has["rout"]:
                        experts(i - 2)
                    if g == 6:
                        if has["emb"]:
                            values(i + 1)
                        if has["rout"]:
                            weights(i - 2, par)
                    if g == 7:
                        if has["emb"]:
                            k_lo(i + 1, 1 - par)
                            q_lo(i + 1, 1 - par, 0)
                        if has["rout"]:
                            places(i - 2, par)
            steps(dve, step)

            ts = S["table_steps"]
            done = [0]

            def then(ins):
                done[0] += 1
                ins.then_inc(ts, 1)
                dve.wait_ge(ts, done[0])
            region = cst[0:1, 2, 0, :]
            then(v.tensor_copy(basu[:], base[0:1, :]))
            then(v.tensor_tensor(cnt[:], base[0:1, :], region, ALU.subtract))
            then(v.tensor_scalar(cni[:, 0], cnt[:], 127.0, None, ALU.add))
            then(v.tensor_scalar(cni[:, 1], cni[:, 0], 7, None, ALU.logical_shift_right))
            then(v.tensor_copy(ntl[:], cni[:, 1]))
            then(v.tensor_copy(cum[:, 0:1], ntl[:, 0:1]))
            for e in range(1, NE):
                then(v.tensor_tensor(cum[:, e:e + 1], cum[:, e - 1:e], ntl[:, e:e + 1], ALU.add))
            then(v.tensor_tensor(adr[:, 0], cum[:], ntl[:], ALU.subtract))
            then(v.tensor_scalar(adr[:, 1], adr[:, 0], -128.0, None, ALU.mult))
            then(v.tensor_tensor(adr[:, 2], adr[:, 1], region, ALU.add))
            then(v.tensor_tensor(adr[:, 0, 0:NE - 1], adr[:, 2, 1:NE], adr[:, 2, 0:NE - 1], ALU.subtract))
            L = NE - 1
            then(v.tensor_tensor(cmp_[:], tio[:, 0].unsqueeze(2).broadcast_to([1, TILES, NE]),
                                 cum[:].unsqueeze(1).broadcast_to([1, TILES, NE]), ALU.is_ge))
            then(v.tensor_tensor(cda[:, :, 0:L], cmp_[:, :, 0:L],
                                 adr[:, 0, 0:L].unsqueeze(1).broadcast_to([1, TILES, L]), ALU.mult))
            then(v.tensor_reduce(tabf[:, 0], cmp_[:, :, 0:L], AX.X, ALU.add))
            then(v.tensor_reduce(tabf[:, 1], cda[:, :, 0:L], AX.X, ALU.add))
            then(v.tensor_tensor(tabf[:, 1], tabf[:, 1], tio[:, 1], ALU.add))
            then(v.tensor_scalar(tabf[:, 2], tabf[:, 1], -1.0, float(DUMMY), ALU.mult, ALU.add))
            then(v.tensor_tensor(tabf[:, 3], tabf[:, 2], cmp_[:, :, L], ALU.mult))
            then(v.tensor_tensor(tabf[:, 1], tabf[:, 1], tabf[:, 3], ALU.add))
            then(v.tensor_copy(tab[:, 0], tabf[:, 0]))
            then(v.tensor_copy(tab[:, 1], tabf[:, 1]))
            v.tensor_copy(hold[0:1], tabf[:, 0, 0:1]).then_inc(S["table_ready"], 1)

            def columns(t, u, e):
                dve.wait_ge(S[f"row{u}"], 4 * (t - u) + 16)
                if not below(t, UP):
                    dve.wait_ge(S[f"out{u}"], 4 * (t - u))
                v.tensor_copy(hold[:], mhalf[:, 0:1])
                v.tensor_copy(cd[:, u, :].unsqueeze(2),
                              XB[:, u, D:ROW].rearrange("p (k e) -> p k e", k=2)[:, :, bass.ds(e, 1)]
                              ).then_inc(S["cols"], 1)
                dve.wait_ge(S["cols"], t + 1)
                v.tensor_copy(du[:, u, :], cd[:, u, 1:2]).then_inc(S["place"], 1)

            def split(t, u):
                dve.wait_ge(S["xa"], t + 1)
                if not below(t, 2):
                    dve.wait_ge(S["hidden_ps"], t - 1)
                v.tensor_copy(xhi[:, u % 2], xa[:, u % 2]).then_inc(S["x_hi"], 1)
                dve.wait_ge(S["x_hi"], t + 1)
                v.tensor_tensor(xlo[:, u % 2], xa[:, u % 2], xhi[:, u % 2].bitcast(f32), ALU.subtract
                                ).then_inc(S["x_lo"], 1)

            def hiddenT(t, u):
                dve.wait_ge(S["hT_ps"], t + 1)
                if not below(t, 2):
                    dve.wait_ge(S["out_ps"], t - 1)
                v.tensor_copy(GT[:, u % 2], PS[:, 4 + u % 2, :]).then_inc(S["hT_sb"], 1)
            slots(dve, TILES, [(2, split), (2, columns), (0, hiddenT)], (columns,))

            def stats_back(k, p):
                if not below(k, UP):
                    dve.wait_ge(S["y3"], k - UP + 1)
                v.tensor_copy(nr3[:, p], kept[:, bass.ds(k, 1)].rearrange("p a n t -> p (a n) t")
                              ).then_inc(S["nr3"], 1)

            def sum3(k, p):
                dve.wait_ge(S[f"in{p}"], 16 * (k - p) + 64)
                v.tensor_tensor(T3[p], RES[p][:, :, 0, :], RES[p][:, :, 1, :], ALU.add).then_inc(S["t3"], 1)
                dve.wait_ge(S["y3"], k + 1)
                dve.wait_ge(S["t3"], 2 * k + 1)
                v.tensor_tensor(T3[p], T3[p], Y3[p], ALU.add).then_inc(S["t3"], 1)
                dve.wait_ge(S["t3"], 2 * k + 2)
                stats(T3[p], mv3[:, p], k, S["bn3"], S["stats3"])

            def output(k, p):
                for t in range(NT):
                    last = v.scalar_tensor_tensor(T3[p][:, t], T3[p][:, t], mv3[:, p, t, 0:1], outg[:],
                                                  ALU.subtract, ALU.mult)
                last.then_inc(S["c3"], 1)
                dve.wait_ge(S["c3"], k + 1)
                dve.wait_ge(S["rstd3"], k + 1)
                dve.wait_ge(S["residual3"], k + 1)
                if not below(k, UP):
                    dve.wait_ge(S[f"st{p}"], 12 * (k - p))
                for t in range(NT):
                    last = v.scalar_tensor_tensor(fin[p][:, t], T3[p][:, t], rs3[:, p, t:t + 1], H3[p][:, t],
                                                  ALU.mult, ALU.add)
                last.then_inc(S["fin"], 1)
            slots(dve, B, [(3, stats_back), (0, sum3), (-1, output)])

        @block.tensor
        def _(pe):
            mm, tr = nc.tensor.matmul, nc.tensor.transpose

            def tok(b, t):
                if t == 0:
                    pe.wait_ge(S["x_loaded"], 96 * (b + 1))
                    if below(b, 1):
                        pe.wait_ge(S["tok_weights"], 16)
                        pe.wait_ge(S["setup_vector"], 1)
                    else:
                        pe.wait_ge(S["vb"], b)
                xv = xt[:].rearrange("p (h w q) -> p h w q", w=HP, q=P16)
                for q in range(QH):
                    last = mm(PS[0:R, MA, t * D:(t + 1) * D], xv[:, t * HP // 2:(t + 1) * HP // 2, :, q],
                              wtok[:, q, :], start=(q == 0), stop=(q == QH - 1))
                if t == 1:
                    last.then_inc(S["tok_ps"], 1)

            def xn_T(b):
                pe.wait_ge(S["xn"], b + 1)
                pe.wait_ge(S["h0"], b + 1)
                for t in range(NT):
                    last = tr(PS[:, MA, t * R:(t + 1) * R], xn[:, t, :], idn[0:R, 0:R])
                last.then_inc(S["xnT_ps"], 1)

            def qk(b, n, m):
                if m == 0:
                    pe.wait_ge(S["xnT_sb"], b + 1)
                    if n == 1:
                        pe.wait_ge(S["rope"], 4 * b + 1)
                elif n == 1:
                    pe.wait_ge(S["rope"], 4 * b + 2)
                elif not below(b, 2):
                    pe.wait_ge(S["h1"], b - 1)
                w_ = (2 * n + m) * D
                mm(PS[:, (MA, MB)[m], 0:NP], wqkv[:, w_:w_ + D], xnT[:], start=True, stop=True
                   ).then_inc(S["qk_ps"], 1)

            def vproj(b):
                pe.wait_ge(S["rope"], 4 * b + 3)
                for t in range(NT):
                    last = mm(PS[0:R, MA, t * D:(t + 1) * D], xnT[:, t * R:(t + 1) * R], wqkv[:, 4 * D:5 * D],
                              start=True, stop=True)
                last.then_inc(S["v_ps"], 1)

            def scores(i, par, g):
                pe.wait_ge(S["q_lo"], NH * i + g + 1)
                if g == 0:
                    pe.wait_ge(S["k_lo"], i + 1)
                for t in range(NT):
                    n = NT * g + t
                    if not (below(i, 1) and g == 0):
                        pe.wait_ge(S["exp"], NH * NT * i + n - NT + 1)
                    rows = slice(t * R, (t + 1) * R)
                    mm(PS[0:R, t, 0:NV], qhi[:, g % QR, rows], khi[:, par, 0:NV], start=True, stop=False)
                    mm(PS[0:R, t, 0:NV], qhi[:, g % QR, rows], klo[:, par, 0:NV], start=False, stop=False)
                    mm(PS[0:R, t, 0:NV], qlo[:, g % QR, rows], khi[:, par, 0:NV], start=False, stop=True
                       ).then_inc(S["scores_ps"], 1)

            def probs_T(i, g, tiles_):
                if 0 in tiles_:
                    pe.wait_ge(S["probs"], NH * i + g + 1)
                for t in tiles_:
                    n = NT * g + t
                    if not (below(i, 1) and n < 2):
                        pe.wait_ge(S["probsT_sb"], NH * NT * i + n - 1)
                    for u in range(NT):
                        last = tr(PS[0:R, TB + n % 2, u * R:(u + 1) * R], E[:, g % 2, u, t * R:(t + 1) * R],
                                  idn[0:R, 0:R])
                    last.then_inc(S["probsT_ps"], 1)

            def weighted(i, g):
                pe.wait_ge(S["probsT_sb"], NT * (NH * i + g + 1))
                pe.wait_ge(S["vp"], NH * i + g + 1)
                if g == 0 and not below(i, 1):
                    pe.wait_ge(S["attn_sb"], i)
                for t in range(NT):
                    last = mm(acc, VP[:, g, t, :], AT[:, g % 2, t, 0:N], start=(g == 0 and t == 0),
                              stop=(g == NH - 1 and t == NT - 1))
                last.then_inc(S["av_ps"], 1)

            def proj(j):
                pe.wait_ge(S["attn_sb"], j + 1)
                if not below(j, 1):
                    pe.wait_ge(S["gate_sb"], j)
                for t in range(NT):
                    last = mm(PS[0:R, MB, t * D:(t + 1) * D], oT[:, t * R:(t + 1) * R], wout[:], start=True, stop=True)
                last.then_inc(S["proj_ps"], 1)

            def x2T_(j, par):
                pe.wait_ge(S["xhat"], j + 1)
                if not below(j, 1):
                    pe.wait_ge(S["pos_read"], j)
                else:
                    pe.wait_ge(S["rope"], 4 * (j + 3))
                for t in range(NT):
                    last = tr(PS[:, MB, t * R:(t + 1) * R], xr[:, par, t, 0:D], idn[0:R, 0:R])
                last.then_inc(S["x2T_ps"], 1)

            def gate(j):
                pe.wait_ge(S["x2T_sb"], j + 1)
                for t in range(NT):
                    last = mm(PS[0:R, MB, t * NE:(t + 1) * NE], x2T[:, t * R:(t + 1) * R], wgate[:],
                              start=True, stop=True)
                last.then_inc(S["gate_ps"], 1)

            def rank(j, emb):
                pe.wait_ge(S["masks"], j + 1)
                if emb:
                    pe.wait_ge(S["rope"], 4 * (j + 4))
                elif below(j, B - 1):
                    pe.wait_ge(S["h1"], j + 2)
                m_, z = msb[:].rearrange("p t e -> p (t e)"), NT * NE
                before, every = trb[:, 0, :], trb[:, 1, :]
                mm(PS[0:R, MB, 0:z], before, m_, start=True, stop=False)
                mm(PS[0:R, MB, NE:z], every, m_[:, 0:2 * NE], start=False, stop=False)
                mm(PS[0:R, MB, 2 * NE:z], every, m_[:, 0:NE], start=False, stop=False)
                for t in range(NT):
                    last = mm(PS[0:R, MB, z:z + NE], every, m_[:, t * NE:(t + 1) * NE], start=False,
                              stop=(t == NT - 1))
                last.then_inc(S["rank_ps"], 1)

            tok(0, 0)
            tok(0, 1)
            pe.wait_ge(S["small_weights"], 16 * NSMALL)
            xn_T(0)
            pe.wait_ge(S["qkv_weights"], 48)
            for n in range(2):
                for m in range(2):
                    qk(0, n, m)
            vproj(0)

            def step(i, par, has):
                emb = has["emb"]
                for g in range(NH):
                    if has["attn"]:
                        scores(i, par, g)
                    if emb:
                        if g < 2:
                            tok(i + 1, g)
                        if g == 3:
                            xn_T(i + 1)
                        if g in (4, 5):
                            qk(i + 1, g - 4, 0)
                            qk(i + 1, g - 4, 1)
                        if g == 6:
                            vproj(i + 1)
                    if has["rout"]:
                        if g == 7:
                            rank(i - 2, emb)
                    if g == 3 and has["res"]:
                        proj(i - 1)
                    if g >= 1 and has["attn"]:
                        probs_T(i, g - 1, (0, 1))
                    if g == 0 and has["res"]:
                        probs_T(i - 1, NH - 1, (0, 1))
                    if g >= 2 and has["attn"]:
                        weighted(i, g - 2)
                    if g < 2 and has["res"]:
                        weighted(i - 1, NH - 2 + g)
                    if g >= 1 and has["attn"]:
                        probs_T(i, g - 1, (2,))
                    if g == 0 and has["res"]:
                        probs_T(i - 1, NH - 1, (2,))
                    if has["rout"]:
                        if g == 0:
                            x2T_(i - 2, par)
                        if g == 1:
                            gate(i - 2)
            steps(pe, step)

            pe.wait_ge(S["table_ready"], 1)
            pe.wait_ge(S["attn_sb"], B)
            pe.wait_ge(S["bias_steps"], 12)

            def rowsT(t, u):
                pe.wait_ge(S[f"row{u}"], 4 * (t - u) + 16)
                if not below(t, 2):
                    pe.wait_ge(S["xa"], t - 1)
                tr(PS[:, u % 2, 0:D], XB[:, u, 0:D], idn[:]).then_inc(S["xT_ps"], 1)

            def hidden(t, u, e):
                pe.wait_ge(S["x_lo"], t + 1)
                if not below(t, 2):
                    pe.wait_ge(S["gelu"], t - 1)
                cols, o = bass.ds(e * FH, FH), PS[:, 2 + u % 2, :]
                mm(o, xhi[:, u % 2], w1hi[:, cols], start=True, stop=False)
                mm(o, xlo[:, u % 2], w1hi[:, cols], start=False, stop=False)
                mm(o, xhi[:, u % 2], w1lo[:, cols], start=False, stop=False)
                mm(o, ones2[:], b1hl[:, cols], start=False, stop=True).then_inc(S["hidden_ps"], 1)

            def hT(t, u):
                pe.wait_ge(S["gelu"], t + 1)
                if not below(t, 2):
                    pe.wait_ge(S["hT_sb"], t - 1)
                for c in range(FC):
                    last = tr(PS[:, 4 + u % 2, c * 128:(c + 1) * 128], hs[:, u % 2, c * 128:(c + 1) * 128], idn[:])
                last.then_inc(S["hT_ps"], 1)

            def second(t, u, e):
                pe.wait_ge(S["hT_sb"], t + 1)
                if not below(t, 2):
                    pe.wait_ge(S["out_sb"], t - 1)
                o = PS[:, 6 + u % 2, 0:D]
                for c in range(FC):
                    mm(o, GT[:, u % 2, c * 128:(c + 1) * 128], w2s[:, bass.ds(e * FH + c * D, D)],
                       start=(c == 0), stop=False)
                mm(o, ones2[:], b2hl[:, bass.ds(e * D, D)], start=False, stop=True).then_inc(S["out_ps"], 1)
            slots(pe, TILES, [(2, rowsT), (1, hidden), (0, hT), (-1, second)], (hidden, second))


def kernel(x, txt, L0_tok_w, L0_tok_b, L0_attn_w_qkv, L0_attn_b_qkv, L0_attn_w_pre, L0_attn_w_post, L0_attn_w_out,
           L0_attn_b_out, L0_ffn_Wg, L0_ffn_W1, L0_ffn_b1, L0_ffn_W2, L0_ffn_b2, L0_ffn_ln_g, L0_ffn_ln_b,
           L0_ffn_out_g, L0_ffn_out_b):
    import concourse.bacc as bacc
    from concourse.bass_utils import run_bass_kernel_spmd

    def a(v):
        return np.asarray(v)

    f = np.float32
    wtok = np.zeros((KR + 1, QH, D), f)
    wtok[:KR] = a(L0_tok_w).reshape(D, C, P16, 2, QH).transpose(3, 1, 2, 4, 0).reshape(KR, QH, D)
    wtok[KR, 0] = a(L0_tok_b)
    partner = np.arange(D) ^ (DH // 4)
    wq, wk, wv = a(L0_attn_w_qkv).reshape(3, D, D)
    bq, bk, bvv = a(L0_attn_b_qkv).reshape(3, D)
    wqkv = np.concatenate([wq.T, wq[partner].T, wk.T, wk[partner].T, wv.T], axis=1)
    bqk = np.stack([bq, bq[partner], bk, bk[partner]], axis=1)
    inv = (1.0 / f(10000.0) ** (np.arange(0, DH, 4, dtype=f) / f(DH))).astype(f)
    pos = np.arange(NP)
    low, chunk = (pos % 64).astype(f), (pos // 64).astype(f)
    rope = np.zeros((D, 2, NP), f)
    for p in range(D):
        d = p % DH
        ang = (low if d < DH // 2 else chunk) * inv[d % 4]
        rope[p, 0] = np.cos(ang)
        rope[p, 1] = np.sin(ang) * (1 if d & 4 else -1)
    consts = np.zeros((R, 4, NT, NE), f)
    token = np.arange(NT)[None, :] * R + np.arange(R)[:, None]
    consts[:, 0] = consts[:, 1] = (token < N)[:, :, None]
    consts[:, 2] = (np.arange(NE) * REGION)[None, None, :]
    consts[:, 3] = 2 * token[:, :, None]
    tri = np.stack([np.triu(np.ones((R, R), f), 1), np.ones((R, R), f)], axis=1)
    tail = np.zeros((128, ROW), f)
    tail[:, D + NE:] = 4 * B * N
    tile_no = np.arange(TILES, dtype=f)

    def rows(vec):
        return np.repeat(a(vec)[None, :], R, axis=0)

    arrays = {
        "x": a(x), "txt": a(txt), "w_tok": wtok, "w_qkvr": wqkv, "b_qkr": bqk, "b_v": rows(bvv),
        "w_pre": np.repeat(a(L0_attn_w_pre).T, DH, axis=0),
        "w_post": np.repeat(np.repeat(a(L0_attn_w_post).T, DH, axis=1)[None], R, axis=0),
        "w_out": a(L0_attn_w_out).T, "b_out": rows(L0_attn_b_out), "w_gate": a(L0_ffn_Wg),
        "w1": a(L0_ffn_W1).transpose(1, 0, 2).reshape(D, NE * FH),
        "b1": np.repeat(a(L0_ffn_b1).reshape(1, NE * FH), 2, axis=0),
        "w2": a(L0_ffn_W2).reshape(NE * FC, 128, D).transpose(1, 0, 2).reshape(128, NE * FC * D),
        "b2": np.repeat(a(L0_ffn_b2).reshape(1, NE * D), 2, axis=0),
        "ln_g": a(L0_ffn_ln_g)[:, None], "ln_b": a(L0_ffn_ln_b)[:, None],
        "out_g": rows(L0_ffn_out_g), "out_b": rows(L0_ffn_out_b),
        "rope": rope, "ident": np.eye(128, dtype=f), "iota": np.repeat(np.arange(NE, dtype=f)[None], R, axis=0),
        "consts": consts, "tri": tri, "pick": np.eye(2, dtype=f), "tail": tail,
        "tiota": np.stack([tile_no, 128 * tile_no])[None],
    }
    nc = bacc.Bacc("TRN2", target_bir_lowering=False, num_devices=1)
    f32 = mybir.dt.float32
    ins, args = {}, []
    for name, v in arrays.items():
        v = np.ascontiguousarray(v)
        ins[f"in_{name}"] = v
        args.append(nc.dram_tensor(f"in_{name}", v.shape, mybir.dt.from_np(v.dtype), kind="ExternalInput").ap())
    for name, shape in (("routed", (DUMMY + 128, ROW)), ("results", (B * N, 2 * D)), ("h1", (B, R, NT * D))):
        args.append(nc.dram_tensor(f"dram_{name}", shape, f32).ap())
    args.append(nc.dram_tensor("out_0", (B, N, D), f32, kind="ExternalOutput").ap())
    early_fusion_kernel(nc, *args)
    r = run_bass_kernel_spmd(nc, [ins], core_ids=[0])
    return r.results[0]["out_0"]
```

```python
import numpy as np
import concourse.bass as bass
from concourse import mybir
from contextlib import ExitStack

B, C, IMG, P16 = 32, 3, 224, 16
HP = IMG // P16
TXT, D, NH, DH = 77, 128, 8, 16
NE, FH = 8, 512
NPATCH = HP * HP
N = NPATCH + TXT
R = NPATCH // 2
NT = 3
NV = N + N % 2
NP = NT * R
FULL = N // 128
RK = 32
NR = NH * RK // 128
AC = NH * FULL + NR
QH = P16 // 2
KR = C * P16 * 2
FC = FH // 128
EPS = 1e-5
ROW = D + 2 * NE
REGION = B * N + 128
TILES = (2 * B * N + NE * 127) // 128
TILES += -TILES % 4
DUMMY = NE * REGION
EB = 4
UP = 4


SMALL = {
    "b_qkr": (D, (4,)),
    "b_v": (128, (D,)),
    "w_pre": (D, (NH,)),
    "w_post": (128, (NH + NR, D)),
    "w_out": (D, (D,)),
    "b_out": (R, (D,)),
    "w_gate": (D, (NE,)),
    "ln_g": (D, (1,)),
    "ln_b": (D, (1,)),
    "out_g": (R, (D,)),
    "out_b": (R, (D,)),
    "ident": (128, (128,)),
    "iota": (R, (NE,)),
    "consts": (R, (4, NT, NE)),
    "tri": (R, (2, R)),
}


def early_fusion_kernel(nc, x, txt, w_tok, w_qkvr, small_in, w1, b12, w2, rope, tail, tiota,
                        routed, results, h1_dram, bias_dram, out):
    f32, f32r, u32, i32, bf16 = (mybir.dt.float32, mybir.dt.float32r, mybir.dt.uint32, mybir.dt.int32,
                                 mybir.dt.bfloat16)
    ALU, ACT, AX = mybir.AluOpType, mybir.ActivationFunctionType, mybir.AxisListType
    ctx = ExitStack()
    with ctx:
        def sb(name, shape, dt=f32):
            return ctx.enter_context(nc.sbuf_tensor(name, shape, dt))

        def sem(name):
            return ctx.enter_context(nc.semaphore(name))

        small = sb("small", list(small_in.shape))
        part, at = {}, 0
        for name, (rows_, shape) in SMALL.items():
            size = int(np.prod(shape))
            part[name] = small[0:rows_, at:at + size]
            if len(shape) > 1:
                axes = " ".join("abc"[:len(shape)])
                part[name] = part[name].rearrange(f"p ({axes}) -> p {axes}", **dict(zip("abc", shape)))
            at += size
        bqk, bv, wpre, wpost, wout, bout, wgate, lng, lnb, outg, outb, idn, iot, cst, trf = (
            part[name] for name in SMALL)
        wtok = sb("wtok", [KR + 1, QH, D])
        wqkv = sb("wqkv", [D, 5 * D])
        w1hi = sb("w1hi", [D, NE * FH], f32r)
        w1lo = sb("w1lo", [D, NE * FH], f32r)
        b1hl = sb("b1hl", [2, NE * FH], f32r)
        w2s = sb("w2s", [128, NE * FC * D])
        b2hl = sb("b2hl", [2, NE * D], f32r)
        cosT = sb("cosT", [D, 2, NP])
        mhalf = sb("mhalf", [R, NT])
        epsT = sb("epsT", [R, NT])
        mone = sb("mone", [R, NT])
        one3 = sb("one3", [R, NT])
        BW = NE * (FH + D) // 128
        bias = sb("bias", [128, BW])
        bias2 = [sb(n, [128, BW], f32r) for n in ("bias_hi", "bias_lo")]
        one2 = sb("one2", [2, 128])
        ones2 = sb("ones2", [2, 128], f32r)
        trb = sb("trb", [R, 2, R], bf16)
        stage = sb("stage", [128, 2, 2048])
        xt = sb("xt", [KR + 1, HP * IMG])
        H0 = sb("H0", [R, NT, D])
        HB = sb("HB", [R, 2, NT, D])
        bst = sb("bst", [R, NT, 6])
        hold = sb("hold", [R, 4])
        holdp = sb("holdp", [R, 2 + UP])
        mv1 = sb("mv1", [R, NT, 2])
        rs1 = sb("rs1", [R, NT])
        xn = sb("xn", [R, NT, D])
        xnT = sb("xnT", [D, NP])
        xnR = sb("xnR", [D, 128 // RK, RK])
        rc = sb("rc", [D, 2, NP])
        rsn = sb("rsn", [D, 2, NP])
        qT = sb("qT", [D, 2, NP])
        kT = sb("kT", [D, NP])
        khi = sb("khi", [D, 2, NP], f32r)
        klo = sb("klo", [D, 2, NP], f32r)
        QR = 2
        qhi = sb("qhi", [D, QR, NP], f32r)
        qlo = sb("qlo", [D, QR, NP], f32r)
        V = sb("V", [128, FULL + 1, D])
        VP = sb("VP", [128, NH, FULL, D])
        VR = sb("VR", [128, NR, D])
        nmax = sb("nmax", [R, NH * NT])
        esum = sb("esum", [R, NH * NT])
        rsum = sb("rsum", [R, NH * NT])
        E = sb("E", [R, EB, NT, NP])
        ER = sb("ER", [R, NR, NT, 128])
        AT = sb("AT", [128, 2, FULL, NP])
        ATR = sb("ATR", [128, NR, NP])
        oT = sb("oT", [D, NP])
        H1 = sb("H1", [R, NT, D])
        mv2 = sb("mv2", [R, NT, 2])
        nr2 = sb("nr2", [R, 2, NT])
        kept = sb("kept", [R, B, 2, NT])
        nm2 = sb("nm2", [R, NT])
        tv2 = sb("tv2", [R, 3, NT])
        rr2 = sb("rr2", [R, NT])
        y2 = sb("y2", [R, NT, D])
        xr = sb("xr", [R, 2, NT, ROW])
        x2T = sb("x2T", [D, NP])
        gl = sb("gl", [R, NT, NE])
        m8 = sb("m8", [R, NT, 8])
        ix8 = sb("ix8", [R, NT, 8], u32)
        ixf = sb("ixf", [R, 2, NT])
        dl = sb("dl", [R, NT])
        ed = sb("ed", [R, NT])
        ed1 = sb("ed1", [R, NT])
        cf = sb("cf", [R, 2, NT])
        eq = sb("eq", [R, 2, NT, NE])
        mk = sb("mk", [R, 2, NT, NE])
        cm = sb("cm", [R, 2, NT, NE])
        ms = sb("ms", [R, NT, NE])
        msb = sb("msb", [R, NT, NE], bf16)
        dd = sb("dd", [R, NT, NE])
        tokb = sb("tokb", [R, NT, NE])
        base = sb("base", [R, NE])
        ps_ = sb("pos", [R, NT, NE])
        sl = sb("sl", [R, 2, NT, NE])
        slf = sb("slf", [R, 2, NT])
        slu = sb("slu", [R, 2, 2, NT], u32)
        cnt = sb("cnt", [1, NE])
        cni = sb("cni", [1, 2, NE], i32)
        ntl = sb("ntl", [1, NE])
        cum = sb("cum", [1, NE])
        adr = sb("adr", [1, 3, NE])
        cmp_, cda = (stage[0:1, i, 0:TILES * NE].rearrange("p (n e) -> p n e", e=NE) for i in range(2))
        tio = sb("tio", [1, 2, TILES])
        tabf = sb("tabf", [1, 4, TILES])
        tab = sb("tab", [1, 2, TILES], u32)
        basu = sb("basu", [1, NE], u32)
        tailt = sb("tailt", [128, ROW])
        XB = sb("XB", [128, UP, ROW])
        xa = sb("xa", [128, 2, D])
        xhi = sb("xhi", [128, 2, D], f32r)
        xlo = sb("xlo", [128, 2, D], f32r)
        hs, GT = (VP[:].rearrange("p (a h) t d -> p a (h t d)", a=2)[:, i].rearrange("p (b n) -> p b n", b=2)
                  for i in range(2))
        cd = sb("cd", [128, UP, 2])
        du = sb("du", [128, UP, 1], u32)
        OT = sb("OT", [128, UP, D])
        w = NT * D

        def parts(buf, count, size, at=0):
            flat = buf[:, at:at + count * size]
            return [flat[:, i * size:(i + 1) * size].rearrange("p (t d) -> p t d", t=NT) for i in range(count)]
        res = parts(stage[0:R].rearrange("p a n -> p (a n)"), UP, 2 * w)
        RES = [a.rearrange("p t (k d) -> p t k d", k=2) for a in res]
        H3, T3 = (parts(w1hi[0:R].bitcast(f32), UP, w, i * UP * w) for i in range(2))
        Y3, fin = (parts(w1lo[0:R].bitcast(f32), UP, w, i * UP * w) for i in range(2))
        nr3 = sb("nr3", [R, UP, 2, NT])
        mv3 = sb("mv3", [R, UP, NT, 2])
        rs3 = sb("rs3", [R, UP, NT])
        nm3 = sb("nm3", [R, UP, NT])

        PS = ctx.enter_context(nc.psum_tensor("PS", [128, 8, 512], f32))
        TB, ACC, MA, MB = 3, 5, 6, 7
        acc = PS[:, ACC, 0:N]

        names = """tok_weights qkv_weights small_weights w1_loaded w2_loaded setup_gpsimd setup_vector vp_rest w1_hi
            weights_rounded bias_in bias_hi bias_lo bias_kept bias_loaded x_loaded txt_loaded kept_h rest av_rest
            tok_ps xnT_ps qk_ps v_ps h0 bn1 bn2 bn3 stats1 stats2 stats3 rstd1 rstd1_steps xn xnT_sb hb rope qk_sb
            k_hi k_lo q_hi q_lo vb vp scores_ps max exp recip probs probsT_ps probsT_sb av_ps attn_sb proj_ps h1
            rstd2 rstd2_steps y2 xhat x2T_ps x2T_sb gate_ps gate_sb top8 logit_gap gap_exp choice_steps masks both
            share_steps routed_cols rank_ps pos_steps pos_read slots scat0 scat1 table_steps table_ready ends_ready
            tails row0 row1 row2 row3 xT_ps xa x_hi x_lo hidden_ps gelu hT_ps hT_sb out_ps out_sb cols place out0
            out1 out2 out3 in0 in1 in2 in3 nr3 y3 t3 rstd3 rstd3_steps carried residual3 c3 g3 fin st0 st1 st2 st3"""
        S = {n: sem(n) for n in names.split()}

        block = ctx.enter_context(nc.Block())

        def below(b, n):
            return isinstance(b, int) and b < n

        def tile_no(i, g, c):
            if g < 0:
                return AC * i - AC + tile_no(0, g + NH, c)
            return AC * i + FULL * g + c + (g * RK) // 128

        def behind(i, g, lag, has):
            if g < lag:
                return (i - 1, g - lag + NH) if has["res"] else None
            return (i, g - lag) if has["attn"] else None

        def rest_no(i, r):
            return AC * i + (AC // NR) * (r + 1) - 1

        def steps(eng, step):
            def peeled(i):
                step(i, i % 2, dict(attn=i < B, emb=i < B - 1, res=1 <= i <= B, rout=i >= 2, late=i >= 3,
                                     load=i < B - 2))
            every = dict(attn=True, emb=True, res=True, rout=True, late=True, load=True)
            for i in range(4):
                peeled(i)
            with eng.Fori(4, B - 3, 2) as i:
                step(i, 0, every)
                step(i + 1, 1, every)
            for i in range(B - 2, B + 2):
                peeled(i)

        def slots(eng, total, stages, by_expert=()):
            ahead = [a for a, _ in stages]

            def expert(t):
                return eng.value_load(tab[0:1, 0, bass.ds(t, 1)], min_val=0, max_val=NE - 1)

            def peeled(s):
                for a, stage_ in stages:
                    if 0 <= s + a < total:
                        stage_(s + a, (s + a) % UP, *([expert(s + a)] if stage_ in by_expert else []))
            for s in range(-max(ahead), 2 * UP):
                peeled(s)
            halves = []
            for h in range(2):
                need = {u + a for a, stage_ in stages if stage_ in by_expert for u in (2 * h, 2 * h + 1)}
                if need:
                    first, count = min(need), max(need) - min(need) + 1
                    regs = [eng.alloc_register(f"expert{h}{n}") for n in range(count)]
                    halves.append((first, regs, {first + n: bass.RuntimeValue.of_register_unchecked(
                        r, min_val=0, max_val=NE - 1) for n, r in enumerate(regs)}))

            def load_experts(h, s):
                if halves:
                    first, regs, _ = halves[h]
                    eng.reg_load(regs, tab[0:1, 0, bass.ds(s + first, len(regs))])
            load_experts(0, 2 * UP)
            with eng.Fori(2 * UP, total - 2 * UP + 1, UP) as s:
                for u in range(UP):
                    if u == 0:
                        load_experts(1, s)
                    if u == 2:
                        load_experts(0, s + UP)
                    for a, stage_ in stages:
                        stage_(s + (u + a), (u + a) % UP,
                               *([halves[u // 2][2][u + a]] if stage_ in by_expert else []))
            for s in range(total - UP, total - min(ahead)):
                peeled(s)

        @block.sync
        def _(sp):
            sp.dma_start(wtok[:], w_tok).then_inc(S["tok_weights"], 16)

            def load(b):
                if not below(b, 1):
                    sp.wait_ge(S["tok_ps"], b)
                for half in range(2):
                    for c in range(C):
                        r0 = half * C * P16 + c * P16
                        dst = xt[r0:r0 + P16, :].rearrange("p (h w) -> p h w", w=IMG)[:, :, 0:IMG - QH * half]
                        src = x[b, c].rearrange("(h p) w -> p h w", p=P16)[:, :, QH * half:IMG]
                        sp.dma_start(dst, src).then_inc(S["x_loaded"], 16)

            def load_txt(b):
                if below(b, 1):
                    sp.wait_ge(S["setup_gpsimd"], 1)
                else:
                    sp.wait_ge(S["xn"], b)
                    sp.wait_ge(S["hb"], b)
                sp.dma_start(H0[0:TXT, 2, :], txt[b]).then_inc(S["txt_loaded"], 16)

            load(0)
            load_txt(0)
            sp.dma_start(wqkv[:], w_qkvr).then_inc(S["qkv_weights"], 16)
            sp.dma_start(cosT[:], rope).then_inc(S["qkv_weights"], 16)
            load(1)
            load_txt(1)

            def step(i, par, has):
                if has["load"]:
                    load(i + 2)
                if has["res"]:
                    sp.wait_ge(S["h1"], i)
                    sp.dma_start(h1_dram[i - 1], H1[:].rearrange("p t d -> p (t d)")).then_inc(S["kept_h"], 16)
                if has["load"]:
                    load_txt(i + 2)
            steps(sp, step)

            sp.wait_ge(S["w2_loaded"], 48)
            sp.wait_ge(S["ends_ready"], 1)
            _, ends = nc.values_load_multi_w_load_instructions(basu[0:1, :], engines=[sp.engine], min_val=0,
                                                               max_val=DUMMY - 128)
            for row in ends:
                sp.dma_start(routed[bass.ds(row, 128), :], tailt[:]).then_inc(S["tails"], 16)
            sp.dma_start(routed[DUMMY:DUMMY + 128, :], tailt[:]).then_inc(S["tails"], 16)
            sp.wait_ge(S["table_ready"], 1)
            sp.wait_ge(S["tails"], 16 * (NE + 1))
            sp.wait_ge(S["scat0"], 48 * B)
            sp.wait_ge(S["scat1"], 48 * B)

            def load_tile(t, u):
                row = sp.value_load(tab[0:1, 1, bass.ds(t, 1)], min_val=0, max_val=DUMMY)
                if not below(t, UP):
                    sp.wait_ge(S["xT_ps"], t - UP + 1)
                    sp.wait_ge(S["cols"], t - UP + 1)
                sp.dma_start(XB[:, u, :], routed[bass.ds(row, 128), :]).then_inc(S[f"row{u}"], 16)
            slots(sp, TILES, [(0, load_tile)])

            for u in range(UP):
                sp.wait_ge(S[f"out{u}"], 16 * (TILES // UP))
            sp.wait_ge(S["kept_h"], 16 * B)

            def load_image(k, p):
                if not below(k, UP):
                    sp.wait_ge(S["fin"], k - UP + 1)
                rows = results[bass.ds(k * N, N), :]
                sp.dma_start(res[p][:, 0:2], rows[0:NPATCH, :].rearrange("(t p) w -> p t w", t=2)
                             ).then_inc(S[f"in{p}"], 16)
                sp.dma_start(res[p][0:TXT, 2], rows[NPATCH:N, :]).then_inc(S[f"in{p}"], 16)
                sp.dma_start(H3[p], h1_dram[k].rearrange("p (t d) -> p t d", t=NT)).then_inc(S[f"in{p}"], 16)

            def store(k, p):
                sp.wait_ge(S["fin"], k + 1)
                sp.dma_start(out[k, 0:NPATCH, :].rearrange("(t p) d -> p t d", t=2), fin[p][:, 0:2, :]
                             ).then_inc(S[f"st{p}"], 16)
                sp.dma_start(out[k, NPATCH:N, :], fin[p][0:TXT, 2, :]).then_inc(S[f"st{p}"], 16)
            slots(sp, B, [(2, load_image), (-2, store)])
            for u in range(UP):
                sp.wait_ge(S[f"st{u}"], 8 * B)

        @block.gpsimd
        def _(pool):
            g_ = nc.gpsimd
            g_.memset(H0[:], 0.0).then_inc(S["setup_gpsimd"], 1)
            g_.memset(E[:], 0.0).then_inc(S["setup_gpsimd"], 1)
            g_.memset(oT[:], 0.0).then_inc(S["setup_gpsimd"], 1)
            g_.memset(mhalf[:], -0.5)
            g_.memset(mone[:], -1.0)
            g_.memset(one3[:], 1.0)
            g_.memset(epsT[:], EPS).then_inc(S["setup_gpsimd"], 1)
            pool.wait_ge(S["bias_lo"], 1)
            for row in range(2):
                for at, cols in ((0, NE * FH), (NE * FH, NE * D)):
                    g_.dma_start(bias_dram[row, at:at + cols].rearrange("(p n) -> p n", p=128),
                                 bias2[row][:, at // 128:(at + cols) // 128]).then_inc(S["bias_kept"], 16)
            pool.wait_ge(S["bias_kept"], 64)
            g_.dma_start(b1hl[:], bias_dram[:, 0:NE * FH]).then_inc(S["bias_loaded"], 16)
            g_.dma_start(b2hl[:], bias_dram[:, NE * FH:]).then_inc(S["bias_loaded"], 16)
            pool.wait_ge(S["small_weights"], 16)
            pool.wait_ge(S["setup_gpsimd"], 4)
            g_.tensor_copy(tokb[:], cst[:, 3])
            g_.tensor_scalar(wpre[:], wpre[:], DH ** -0.5, None, ALU.mult).then_inc(S["setup_gpsimd"], 1)

            def carry_wait(c):
                return g_.tensor_tensor(holdp[:, c:c + 1], epsT[:, 0:1], epsT[:, 0:1], ALU.add)

            def norm1(b):
                pool.wait_ge(S["stats1"], b + 1)
                g_.tensor_tensor(rs1[:], mv1[:, :, 1], epsT[:], ALU.add).then_inc(S["rstd1_steps"], 1)
                pool.wait_ge(S["rstd1_steps"], b + 1)
                g_.tensor_tensor(rs1[:], rs1[:], mhalf[:], ALU.pow).then_inc(S["rstd1"], 1)

            def hb(b, par):
                pool.wait_ge(S["h0"], b + 1)
                pool.wait_ge(S["txt_loaded"], 16 * (b + 1))
                if not below(b, 2):
                    pool.wait_ge(S["h1"], b - 1)
                g_.tensor_tensor(HB[:, par], H0[:], bout[:].unsqueeze(1).broadcast_to([R, NT, D]),
                                 ALU.add).then_inc(S["hb"], 1)

            def rope_add(b, par, n):
                pool.wait_ge(S["rope"], 4 * b + 2 * n + 2)
                if n == 0:
                    if not below(b, 2):
                        pool.wait_ge(S["q_lo"], NH * (b - 1))
                    dst = qT[:, par]
                else:
                    if not below(b, 1):
                        pool.wait_ge(S["k_hi"], b)
                        pool.wait_ge(S["k_lo"], b)
                    dst = kT[:]
                g_.tensor_tensor(dst, rc[:, n, :], rsn[:, n, :], ALU.add).then_inc(S["qk_sb"], 1)

            def vpost(b, heads):
                pool.wait_ge(S["vb"], b + 1)
                for h in heads:
                    if not below(b, 1):
                        pool.wait_ge(S["av_ps"], NH * (b - 1) + h + 1)
                    g_.tensor_tensor(VP[:, h], V[:, 0:FULL], wpost[:, h, :].unsqueeze(1).broadcast_to([128, FULL, D]),
                                     ALU.mult).then_inc(S["vp"], 1)

            def vpost_rest(b, r):
                pool.wait_ge(S["vb"], b + 1)
                if not below(b, 1):
                    pool.wait_ge(S["av_rest"], NR * (b - 1) + r + 1)
                g_.tensor_tensor(VR[:, r], V[:, FULL], wpost[:, NH + r], ALU.mult).then_inc(S["vp_rest"], 1)

            def rest(i, g):
                pool.wait_ge(S["recip"], NH * i + g + 1)
                r, at = g * RK // 128, g * RK % 128
                if at == 0 and not below(i, 1):
                    pool.wait_ge(S["probsT_ps"], AC * (i - 1) + (AC // NR) * (r + 1))
                g_.tensor_tensor(ER[:, r, :, at:at + RK], E[:, g % EB, :, FULL * 128:FULL * 128 + RK],
                                 rsum[:, NT * g:NT * g + NT].unsqueeze(2).broadcast_to([R, NT, RK]), ALU.mult
                                 ).then_inc(S["rest"], 1)

            def norm2(b):
                st = S["rstd2_steps"]
                pool.wait_ge(S["stats2"], b + 1)
                g_.tensor_tensor(tv2[:, 0], mv2[:, :, 1], epsT[:], ALU.add).then_inc(st, 1)
                pool.wait_ge(st, 6 * b + 1)
                g_.tensor_tensor(nr2[:, 0], tv2[:, 0], mhalf[:], ALU.pow).then_inc(st, 1)
                pool.wait_ge(st, 6 * b + 2)
                g_.tensor_tensor(nm2[:], mv2[:, :, 0], nr2[:, 0], ALU.mult)
                g_.tensor_tensor(tv2[:, 1], mv2[:, :, 1], nr2[:, 0], ALU.mult).then_inc(st, 1)
                pool.wait_ge(st, 6 * b + 3)
                g_.tensor_tensor(nr2[:, 1], nm2[:], mone[:], ALU.mult).then_inc(S["rstd2"], 1)
                g_.tensor_tensor(tv2[:, 2], tv2[:, 1], nr2[:, 0], ALU.mult).then_inc(st, 1)
                pool.wait_ge(st, 6 * b + 4)
                g_.tensor_tensor(tv2[:, 0], tv2[:, 2], epsT[:], ALU.add).then_inc(st, 1)
                pool.wait_ge(st, 6 * b + 5)
                g_.tensor_tensor(rr2[:], tv2[:, 0], mhalf[:], ALU.pow).then_inc(st, 1)

            def shares(j):
                st = S["share_steps"]
                pool.wait_ge(S["gap_exp"], j + 1)
                g_.tensor_tensor(ed1[:], ed[:], one3[:], ALU.add).then_inc(st, 1)
                pool.wait_ge(st, 5 * j + 1)
                g_.tensor_tensor(cf[:, 0, :], ed1[:], mone[:], ALU.pow).then_inc(st, 1)
                pool.wait_ge(st, 5 * j + 2)
                g_.tensor_tensor(cf[:, 1, :], ed[:], cf[:, 0, :], ALU.mult).then_inc(st, 1)

            def both_masks(j):
                st = S["share_steps"]
                pool.wait_ge(S["masks"], j + 1)
                g_.tensor_tensor(msb[:], mk[:, 0], mk[:, 1], ALU.add).then_inc(S["both"], 1)
                g_.tensor_tensor(ms[:], mk[:, 0], mk[:, 1], ALU.add).then_inc(st, 1)
                pool.wait_ge(st, 5 * j + 4)
                g_.tensor_tensor(cm[:].rearrange("p k t e -> p (k t) e"), mk[:].rearrange("p k t e -> p (k t) e"),
                                 cf[:].rearrange("p k t -> p (k t)").unsqueeze(2).broadcast_to([R, 2 * NT, NE]),
                                 ALU.mult)
                g_.tensor_tensor(dd[:], ms[:], tokb[:], ALU.mult).then_inc(st, 1)

            def routed_columns(j, par):
                pool.wait_ge(S["share_steps"], 5 * j + 5)
                pool.wait_ge(S["xhat"], j + 1)
                g_.tensor_tensor(xr[:, par, :, D:D + NE], cm[:, 0], cm[:, 1], ALU.add)
                g_.tensor_tensor(xr[:, par, :, D + NE:ROW], dd[:], mk[:, 1], ALU.add)
                g_.tensor_scalar(tokb[:], tokb[:], 2.0 * N, None, ALU.add).then_inc(S["routed_cols"], 1)

            def scatter(j, par, k):
                if k == 0:
                    pool.wait_ge(S["slots"], j + 1)
                    pool.wait_ge(S["xhat"], j + 1)
                    carry_wait(par)
                for t in range(NT):
                    rows = R if t < 2 else TXT
                    g_.indirect_dma_start(
                        out=routed, out_offset=bass.IndirectOffsetOnAxis(ap=slu[0:rows, par, k, t:t + 1], axis=0),
                        in_=xr[0:rows, par, t, :], in_offset=None).then_inc(S[f"scat{par}"], 16)

            norm1(0)
            hb(0, 0)
            rope_add(0, 0, 0)
            rope_add(0, 0, 1)
            vpost(0, range(4))
            vpost_rest(0, 0)

            def step(i, par, has):
                for g in range(NH):
                    head = behind(i, g, 1, has)
                    if head:
                        rest(*head)
                    if g == (0 if has["res"] else 7) and has["late"]:
                        scatter(i - 3, 1 - par, 0)
                    if g == (1 if has["res"] else 7) and has["late"]:
                        scatter(i - 3, 1 - par, 1)
                    if g == 2:
                        if has["emb"]:
                            norm1(i + 1)
                        if has["attn"]:
                            vpost(i, (4, 5))
                    if g == 3 and has["attn"]:
                        vpost(i, (6, 7))
                        vpost_rest(i, 1)
                    if g == 4 and has["res"]:
                        norm2(i - 1)
                    if g == 5:
                        if has["emb"]:
                            rope_add(i + 1, 1 - par, 0)
                    if g == 6:
                        if has["emb"]:
                            rope_add(i + 1, 1 - par, 1)
                        if has["rout"]:
                            shares(i - 2)
                            both_masks(i - 2)
                            routed_columns(i - 2, par)
                    if g == 7 and has["emb"]:
                        vpost(i + 1, range(4))
                        vpost_rest(i + 1, 0)
                        hb(i + 1, 1 - par)
            steps(pool, step)
            scatter(B - 1, 1, 0)
            scatter(B - 1, 1, 1)

            def scatter_out(t, u):
                if not below(t, UP):
                    pool.wait_ge(S["carried"], t - UP + 1)
                pool.wait_ge(S["out_sb"], t + 1)
                pool.wait_ge(S["place"], t + 1)
                carry_wait(2 + u).then_inc(S["carried"], 1)
                g_.indirect_dma_start(
                    out=results.rearrange("n (k d) -> (n k) d", k=2),
                    out_offset=bass.IndirectOffsetOnAxis(ap=du[:, u, :], axis=0), in_=OT[:, u, :], in_offset=None,
                    bounds_check=2 * B * N - 1, oob_is_err=False).then_inc(S[f"out{u}"], 16)
            slots(pool, TILES, [(0, scatter_out)])

            def residual3(k, p):
                pool.wait_ge(S["y3"], k + 1)
                g_.tensor_tensor(H3[p], H3[p], outb[:].unsqueeze(1).broadcast_to([R, NT, D]), ALU.add
                                 ).then_inc(S["residual3"], 1)

            def norm3(k, p):
                pool.wait_ge(S["stats3"], k + 1)
                st = S["rstd3_steps"]
                g_.tensor_tensor(nm3[:, p], mv3[:, p, :, 0], mone[:], ALU.mult)
                g_.tensor_tensor(rs3[:, p], mv3[:, p, :, 1], epsT[:], ALU.add).then_inc(st, 1)
                pool.wait_ge(st, 2 * k + 1)
                g_.tensor_tensor(rs3[:, p], rs3[:, p], mhalf[:], ALU.pow).then_inc(st, 1)
                pool.wait_ge(st, 2 * k + 2)
                g_.tensor_tensor(nm3[:, p], nm3[:, p], rs3[:, p], ALU.mult).then_inc(S["rstd3"], 1)
            slots(pool, B, [(0, norm3), (0, residual3)])

        @block.scalar
        def _(act):
            act.dma_start(bias[:], b12).then_inc(S["bias_in"], 16)
            act.dma_start(small[:], small_in).then_inc(S["small_weights"], 16)
            act.wait_ge(S["x_loaded"], 96)
            for a in range(2):
                act.dma_start(stage[:, a, :], w1[:, a * 2048:(a + 1) * 2048]).then_inc(S["w1_loaded"], 16)
            for dst, src in ((w2s, w2), (tio, tiota), (tailt, tail)):
                act.dma_start(dst[:], src).then_inc(S["w2_loaded"], 16)

            def q_hi(i, par, g):
                act.wait_ge(S["qk_sb"], 2 * i + 1)
                if below(i, 1) and g == 0:
                    act.wait_ge(S["setup_gpsimd"], 5)
                if not (below(i, 1) and g < QR):
                    act.wait_ge(S["scores_ps"], NT * (NH * i + g - QR + 1))
                nc.scalar.activation(qhi[:, g % QR, :], qT[:, par, :], ACT.Copy, scale=wpre[:, g:g + 1]
                                     ).then_inc(S["q_hi"], 1)

            def probs(i, g):
                for t in range(NT):
                    n = NT * g + t
                    act.wait_ge(S["max"], NH * NT * i + n + 1)
                    if t == 0:
                        if below(i, 1) and g < EB:
                            act.wait_ge(S["setup_gpsimd"], 4)
                        else:
                            act.wait_ge(S["probsT_ps"], tile_no(i, g - EB, FULL - 1) + 1)
                            act.wait_ge(S["rest"], NH * i + g - EB + 1)
                    nc.scalar.activation(E[:, g % EB, t, 0:N], PS[0:R, t, 0:N], ACT.Exp, bias=nmax[:, n:n + 1],
                                         accum_out=esum[:, n:n + 1]).then_inc(S["exp"], 1)

            def probsT(i, g):
                for c in range(FULL):
                    n = tile_no(i, g, c)
                    act.wait_ge(S["probsT_ps"], n + 1)
                    if c == 0 and not (below(i, 1) and g < 2):
                        act.wait_ge(S["av_ps"], NH * i + g - 1)
                    nc.scalar.copy(AT[:, g % 2, c, :], PS[:, TB + tile_no(0, g, c) % 2, 0:NP]
                                   ).then_inc(S["probsT_sb"], 1)

            def restT(i, r):
                act.wait_ge(S["probsT_ps"], rest_no(i, r) + 1)
                if not below(i, 1):
                    act.wait_ge(S["av_rest"], NR * (i - 1) + r + 1)
                nc.scalar.copy(ATR[:, r, :], PS[:, TB + rest_no(0, r) % 2, 0:NP]).then_inc(S["probsT_sb"], 1)

            def attn_out(i):
                act.wait_ge(S["av_rest"], NR * (i + 1))
                if below(i, 1):
                    act.wait_ge(S["setup_gpsimd"], 4)
                else:
                    act.wait_ge(S["proj_ps"], i)
                nc.scalar.copy(oT[:, 0:N], acc).then_inc(S["attn_sb"], 1)

            def normedT(b):
                act.wait_ge(S["xnT_ps"], b + 1)
                if not below(b, 1):
                    act.wait_ge(S["v_ps"], b)
                nc.scalar.copy(xnR[:], PS[:, MA, FULL * 128:FULL * 128 + RK].unsqueeze(1).broadcast_to(
                    [D, 128 // RK, RK]))
                nc.scalar.copy(xnT[:], PS[:, MA, 0:NP]).then_inc(S["xnT_sb"], 1)

            def x2_T(j):
                act.wait_ge(S["x2T_ps"], j + 1)
                if not below(j, 1):
                    act.wait_ge(S["gate_ps"], j)
                nc.scalar.activation(x2T[:], PS[:, MB, 0:NP], ACT.Identity, bias=lnb[:, 0:1], scale=lng[:, 0:1]
                                     ).then_inc(S["x2T_sb"], 1)

            def k_hi(b, par):
                act.wait_ge(S["qk_sb"], 2 * b + 2)
                if not below(b, 2):
                    act.wait_ge(S["scores_ps"], NH * NT * (b - 1))
                nc.scalar.copy(khi[:, par], kT[:]).then_inc(S["k_hi"], 1)

            def normed2(j):
                act.wait_ge(S["rstd2"], j + 1)
                if not below(j, 1):
                    act.wait_ge(S["xhat"], j)
                for t in range(NT):
                    last = nc.scalar.activation(y2[:, t, :], H1[:, t, :], ACT.Identity, bias=nr2[:, 1, t:t + 1],
                                                scale=nr2[:, 0, t:t + 1])
                last.then_inc(S["y2"], 1)

            def xhat(j, par):
                act.wait_ge(S["y2"], j + 1)
                act.wait_ge(S["rstd2_steps"], 6 * j + 6)
                if not below(j, 2):
                    act.wait_ge(S[f"scat{par}"], 48 * (j - par))
                for t in range(NT):
                    last = nc.scalar.activation(xr[:, par, t, 0:D], y2[:, t, :], ACT.Copy, scale=rr2[:, t:t + 1])
                last.then_inc(S["xhat"], 1)

            normedT(0)
            k_hi(0, 0)
            q_hi(0, 0, 0)
            q_hi(0, 0, 1)

            def step(i, par, has):
                for g in range(NH):
                    if has["attn"]:
                        probs(i, g)
                    head = behind(i, g, 2, has)
                    if head:
                        probsT(*head)
                        if head[1] % 4 == 3:
                            restT(head[0], head[1] // 4)
                    if g == 2 and has["res"]:
                        attn_out(i - 1)
                    if g < NH - 2 and has["attn"]:
                        q_hi(i, par, g + 2)
                    if g >= NH - 2 and has["emb"]:
                        q_hi(i + 1, 1 - par, g + 2 - NH)
                    if g == 5 and has["rout"]:
                        act.wait_ge(S["logit_gap"], i - 1)
                        nc.scalar.activation(ed[:], dl[:], ACT.Exp).then_inc(S["gap_exp"], 1)
                    if g == 0 and has["rout"]:
                        x2_T(i - 2)
                    if g == 3 and has["emb"]:
                        normedT(i + 1)
                    if g == 5 and has["res"]:
                        normed2(i - 1)
                    if g == 6 and has["emb"]:
                        k_hi(i + 1, 1 - par)
                    if g == 7 and has["res"]:
                        xhat(i - 1, 1 - par)
            steps(act, step)

            def affine(t, u):
                act.wait_ge(S["xT_ps"], t + 1)
                if not below(t, 2):
                    act.wait_ge(S["x_lo"], t - 1)
                nc.scalar.activation(xa[:, u % 2], PS[:, u % 2, 0:D], ACT.Identity, bias=lnb[:, 0:1],
                                     scale=lng[:, 0:1]).then_inc(S["xa"], 1)

            def gelu(t, u):
                act.wait_ge(S["hidden_ps"], t + 1)
                if not below(t, 2):
                    act.wait_ge(S["hT_ps"], t - 1)
                nc.scalar.activation(hs[:, u % 2], PS[:, 2 + u % 2, :], ACT.Gelu_apprx_tanh).then_inc(S["gelu"], 1)

            def result(t, u):
                act.wait_ge(S["out_ps"], t + 1)
                act.wait_ge(S["cols"], t + 1)
                if not below(t, UP):
                    act.wait_ge(S[f"out{u}"], 4 * (t - u))
                nc.scalar.activation(OT[:, u], PS[:, 6 + u % 2, 0:D], ACT.Copy, scale=cd[:, u, 0:1]
                                     ).then_inc(S["out_sb"], 1)
            slots(act, TILES, [(2, affine), (1, gelu), (-1, result)])

            def normed3(k, p):
                act.wait_ge(S["nr3"], k + 1)
                act.wait_ge(S[f"in{p}"], 12 * (k - p) + 48)
                if not below(k, UP):
                    act.wait_ge(S["t3"], 2 * (k - UP + 1))
                for t in range(NT):
                    last = nc.scalar.activation(Y3[p][:, t], H3[p][:, t], ACT.Identity, bias=nr3[:, p, 1, t:t + 1],
                                                scale=nr3[:, p, 0, t:t + 1])
                last.then_inc(S["y3"], 1)

            def scale3(k, p):
                act.wait_ge(S["rstd3"], k + 1)
                for t in range(NT):
                    last = nc.scalar.activation(T3[p][:, t], T3[p][:, t], ACT.Identity, bias=nm3[:, p, t:t + 1],
                                                scale=rs3[:, p, t:t + 1])
                last.then_inc(S["c3"], 1)
            slots(act, B, [(0, normed3), (-1, scale3)])

        @block.vector
        def _(dve):
            v = nc.vector
            v.memset(xt[KR:KR + 1, :], 1.0).then_inc(S["setup_vector"], 1)
            v.memset(one2[:], 1.0).then_inc(S["setup_vector"], 1)
            dve.wait_ge(S["setup_vector"], 2)
            v.tensor_copy(ones2[:], one2[:])
            dve.wait_ge(S["bias_in"], 16)
            v.tensor_copy(bias2[0][:], bias[:]).then_inc(S["bias_hi"], 1)
            dve.wait_ge(S["bias_hi"], 1)
            v.tensor_tensor(bias2[1][:], bias[:], bias2[0][:].bitcast(f32), ALU.subtract).then_inc(S["bias_lo"], 1)
            dve.wait_ge(S["small_weights"], 16)
            v.tensor_copy(trb[:], trf[:])
            v.tensor_copy(base[:], cst[:, 2, 0, :])

            def stats(src, mv, b, bn, done):
                for t in range(NT):
                    last = v.bn_stats(bst[:, t, :], src[:, t, :])
                last.then_inc(bn, 1)
                dve.wait_ge(bn, b + 1)
                v.tensor_copy(hold[:, 0:1], bst[:, 0, 0:1])
                for t in range(NT):
                    last = v.bn_aggr(mv[:, t, :], bst[:, t, :])
                last.then_inc(done, 1)

            def token_stats(b):
                dve.wait_ge(S["tok_ps"], b + 1)
                if below(b, 1):
                    dve.wait_ge(S["setup_gpsimd"], 4)
                else:
                    dve.wait_ge(S["hb"], b)
                v.tensor_copy(H0[:, 0:2, :], PS[0:R, MA, 0:2 * D].rearrange("p (t d) -> p t d", t=2)
                              ).then_inc(S["h0"], 1)
                dve.wait_ge(S["txt_loaded"], 16 * (b + 1))
                dve.wait_ge(S["h0"], b + 1)
                stats(H0, mv1, b, S["bn1"], S["stats1"])

            def normed(b):
                dve.wait_ge(S["rstd1"], b + 1)
                if not below(b, 1):
                    dve.wait_ge(S["xnT_ps"], b)
                for t in range(NT):
                    last = v.tensor_scalar(xn[:, t, :], H0[:, t, :], mv1[:, t, 0:1], rs1[:, t:t + 1],
                                           ALU.subtract, ALU.mult)
                last.then_inc(S["xn"], 1)

            def rope_mul(b, n):
                for m, (dst, bank) in enumerate(((rc, MA), (rsn, MB))):
                    dve.wait_ge(S["qk_ps"], 4 * b + 2 * n + m + 1)
                    if m == 0 and not below(b, 1):
                        dve.wait_ge(S["qk_sb"], 2 * b - 1 + n)
                    v.scalar_tensor_tensor(dst[:, n, :], PS[:, bank, 0:NP], bqk[:, 2 * n + m:2 * n + m + 1],
                                           cosT[:, m, :], ALU.add, ALU.mult).then_inc(S["rope"], 1)

            def values(b):
                dve.wait_ge(S["v_ps"], b + 1)
                if not below(b, 1):
                    dve.wait_ge(S["vp"], NH * b)
                    dve.wait_ge(S["vp_rest"], NR * b)
                v.tensor_tensor(V[:], PS[:, MA, 0:(FULL + 1) * D].rearrange("p (t d) -> p t d", d=D),
                                bv[:].unsqueeze(1).broadcast_to([128, FULL + 1, D]), ALU.add).then_inc(S["vb"], 1)

            def q_lo(i, par, g):
                dve.wait_ge(S["q_hi"], NH * i + g + 1)
                dve.wait_ge(S["qk_sb"], 2 * i + 1)
                v.scalar_tensor_tensor(qlo[:, g % QR, :], qT[:, par, :], wpre[:, g:g + 1],
                                       qhi[:, g % QR, :].bitcast(f32), ALU.mult, ALU.subtract).then_inc(S["q_lo"], 1)

            def k_lo(b, par):
                dve.wait_ge(S["k_hi"], b + 1)
                v.tensor_tensor(klo[:, par], kT[:], khi[:, par].bitcast(f32), ALU.subtract).then_inc(S["k_lo"], 1)

            def row_sums(i, g):
                dve.wait_ge(S["exp"], NT * (NH * i + g + 1))
                v.reciprocal(rsum[:, NT * g:NT * g + NT], esum[:, NT * g:NT * g + NT]).then_inc(S["recip"], 1)

            def head_probs(i, g):
                dve.wait_ge(S["recip"], NH * i + g + 1)
                for t in range(NT):
                    last = v.tensor_scalar(E[:, g % EB, t, 0:FULL * 128], E[:, g % EB, t, 0:FULL * 128],
                                           rsum[:, NT * g + t:NT * g + t + 1], None, ALU.mult)
                last.then_inc(S["probs"], 1)

            def head_max(i, g):
                for t in range(NT):
                    n = NT * g + t
                    dve.wait_ge(S["scores_ps"], NH * NT * i + n + 1)
                    v.tensor_reduce(nmax[:, n:n + 1], PS[0:R, t, 0:N], AX.X, ALU.max, negate=True
                                    ).then_inc(S["max"], 1)

            def residual(j, par):
                dve.wait_ge(S["proj_ps"], j + 1)
                dve.wait_ge(S["hb"], j + 1)
                if not below(j, 1):
                    dve.wait_ge(S["y2"], j)
                    dve.wait_ge(S["kept_h"], 16 * j)
                v.tensor_tensor(H1[:], PS[0:R, MB, 0:NT * D].rearrange("p (t d) -> p t d", t=NT), HB[:, par],
                                ALU.add).then_inc(S["h1"], 1)
                dve.wait_ge(S["h1"], j + 1)
                stats(H1, mv2, j, S["bn2"], S["stats2"])

            def keep(j):
                dve.wait_ge(S["rstd2"], j + 1)
                v.tensor_copy(kept[:, bass.ds(j, 1)].rearrange("p a n t -> p (a n) t"), nr2[:])

            def logits(j):
                dve.wait_ge(S["gate_ps"], j + 1)
                v.tensor_copy(gl[:], PS[0:R, MB, 0:NT * NE].rearrange("p (t e) -> p t e", t=NT)
                              ).then_inc(S["gate_sb"], 1)

            def top(j):
                dve.wait_ge(S["gate_sb"], j + 1)
                v.tensor_copy(hold[:, 1:2], gl[:, 0, 0:1])
                for t in range(NT):
                    last = v.max(m8[:, t, :], gl[:, t, :])
                last.then_inc(S["top8"], 1)
                dve.wait_ge(S["top8"], j + 1)
                v.tensor_tensor(dl[:], m8[:, :, 1], m8[:, :, 0], ALU.subtract).then_inc(S["logit_gap"], 1)
                for t in range(NT):
                    last = v.max_index(ix8[:, t, :], m8[:, t, :], gl[:, t, :])
                last.then_inc(S["choice_steps"], 1)

            def experts(j):
                cs = S["choice_steps"]
                dve.wait_ge(cs, 3 * j + 1)
                v.tensor_copy(ixf[:].rearrange("p k t -> p t k"), ix8[:, :, 0:2]).then_inc(cs, 1)
                dve.wait_ge(cs, 3 * j + 2)
                v.tensor_tensor(eq[:].rearrange("p k t e -> p (k t) e"),
                                iot[:].unsqueeze(1).broadcast_to([R, 2 * NT, NE]),
                                ixf[:].rearrange("p k t -> p (k t)").unsqueeze(2).broadcast_to([R, 2 * NT, NE]),
                                ALU.is_equal).then_inc(cs, 1)
                dve.wait_ge(cs, 3 * j + 3)
                v.tensor_tensor(mk[:], eq[:], cst[:, 0:2], ALU.mult).then_inc(S["masks"], 1)

            def places(j, par):
                st = S["pos_steps"]
                dve.wait_ge(S["rank_ps"], j + 1)
                dve.wait_ge(S["routed_cols"], j + 1)
                v.tensor_tensor(ps_[:], PS[0:R, MB, 0:NT * NE].rearrange("p (t e) -> p t e", t=NT),
                                base[:].unsqueeze(1).broadcast_to([R, NT, NE]), ALU.add).then_inc(st, 1)
                dve.wait_ge(st, 3 * j + 1)
                for k in range(2):
                    v.tensor_tensor(sl[:, k], mk[:, k], ps_[:], ALU.mult)
                v.tensor_tensor(base[:], PS[0:R, MB, NT * NE:(NT + 1) * NE], base[:], ALU.add
                                ).then_inc(S["pos_read"], 1)
                dve.wait_ge(S["pos_read"], j + 1)
                v.tensor_reduce(slf[:], sl[:], AX.X, ALU.add).then_inc(st, 1)
                dve.wait_ge(st, 3 * j + 2)
                v.tensor_copy(slu[:, par], slf[:]).then_inc(st, 1)
                dve.wait_ge(st, 3 * j + 3)
                v.tensor_copy(hold[:, 2:3], slf[:, 0, 0:1]).then_inc(S["slots"], 1)

            token_stats(0)
            normed(0)
            rope_mul(0, 0)
            rope_mul(0, 1)
            values(0)
            k_lo(0, 0)
            q_lo(0, 0, 0)
            dve.wait_ge(S["w1_loaded"], 32)
            for a in range(2):
                v.tensor_copy(w1hi[:, a * 2048:(a + 1) * 2048], stage[:, a, :]).then_inc(S["w1_hi"], 1)
            for a in range(2):
                dve.wait_ge(S["w1_hi"], a + 1)
                v.tensor_tensor(w1lo[:, a * 2048:(a + 1) * 2048], stage[:, a, :],
                                w1hi[:, a * 2048:(a + 1) * 2048].bitcast(f32),
                                ALU.subtract).then_inc(S["weights_rounded"], 1)

            def step(i, par, has):
                for g in range(NH):
                    if has["attn"]:
                        head_max(i, g)
                    head = behind(i, g, 1, has)
                    if head:
                        row_sums(*head)
                    if has["attn"] and g < NH - 1:
                        q_lo(i, par, g + 1)
                    if g == 7 and has["emb"]:
                        k_lo(i + 1, 1 - par)
                        q_lo(i + 1, 1 - par, 0)
                    if head:
                        head_probs(*head)
                    if has["emb"]:
                        if g == 1:
                            token_stats(i + 1)
                        if g == 2:
                            normed(i + 1)
                        if g in (4, 5):
                            rope_mul(i + 1, g - 4)
                        if g == 6:
                            values(i + 1)
                    if g == 3 and has["res"]:
                        residual(i - 1, 1 - par)
                    if has["rout"]:
                        if g == 0:
                            keep(i - 2)
                        if g == 2:
                            logits(i - 2)
                        if g == 5:
                            top(i - 2)
                        if g == 6:
                            experts(i - 2)
                        if g == 7:
                            places(i - 2, par)
            steps(dve, step)

            ts = S["table_steps"]
            done = [0]

            def then(ins):
                done[0] += 1
                ins.then_inc(ts, 1)
                dve.wait_ge(ts, done[0])
            region = cst[0:1, 2, 0, :]
            dve.wait_ge(S["w2_loaded"], 48)
            v.tensor_copy(basu[:], base[0:1, :]).then_inc(S["ends_ready"], 1)
            then(v.tensor_tensor(cnt[:], base[0:1, :], region, ALU.subtract))
            then(v.tensor_scalar(cni[:, 0], cnt[:], 127.0, None, ALU.add))
            then(v.tensor_scalar(cni[:, 1], cni[:, 0], 7, None, ALU.logical_shift_right))
            then(v.tensor_copy(ntl[:], cni[:, 1]))
            then(v.tensor_copy(cum[:, 0:1], ntl[:, 0:1]))
            for e in range(1, NE):
                then(v.tensor_tensor(cum[:, e:e + 1], cum[:, e - 1:e], ntl[:, e:e + 1], ALU.add))
            then(v.tensor_tensor(adr[:, 0], cum[:], ntl[:], ALU.subtract))
            then(v.tensor_scalar(adr[:, 1], adr[:, 0], -128.0, None, ALU.mult))
            then(v.tensor_tensor(adr[:, 2], adr[:, 1], region, ALU.add))
            then(v.tensor_tensor(adr[:, 0, 0:NE - 1], adr[:, 2, 1:NE], adr[:, 2, 0:NE - 1], ALU.subtract))
            L = NE - 1
            then(v.tensor_tensor(cmp_[:], tio[:, 0].unsqueeze(2).broadcast_to([1, TILES, NE]),
                                 cum[:].unsqueeze(1).broadcast_to([1, TILES, NE]), ALU.is_ge))
            then(v.tensor_tensor(cda[:, :, 0:L], cmp_[:, :, 0:L],
                                 adr[:, 0, 0:L].unsqueeze(1).broadcast_to([1, TILES, L]), ALU.mult))
            then(v.tensor_reduce(tabf[:, 0], cmp_[:, :, 0:L], AX.X, ALU.add))
            then(v.tensor_reduce(tabf[:, 1], cda[:, :, 0:L], AX.X, ALU.add))
            then(v.tensor_tensor(tabf[:, 1], tabf[:, 1], tio[:, 1], ALU.add))
            then(v.tensor_scalar(tabf[:, 2], tabf[:, 1], -1.0, float(DUMMY), ALU.mult, ALU.add))
            then(v.tensor_tensor(tabf[:, 3], tabf[:, 2], cmp_[:, :, L], ALU.mult))
            then(v.tensor_tensor(tabf[:, 1], tabf[:, 1], tabf[:, 3], ALU.add))
            then(v.tensor_copy(tab[:, 0], tabf[:, 0]))
            then(v.tensor_copy(tab[:, 1], tabf[:, 1]))
            v.tensor_copy(hold[0:1, 3:4], tabf[:, 0, 0:1]).then_inc(S["table_ready"], 1)

            def columns(t, u, e):
                dve.wait_ge(S[f"row{u}"], 4 * (t - u) + 16)
                if not below(t, UP):
                    dve.wait_ge(S[f"out{u}"], 4 * (t - u))
                v.tensor_copy(hold[:, 3:4], mhalf[:, 0:1])
                v.tensor_copy(cd[:, u, :].unsqueeze(2),
                              XB[:, u, D:ROW].rearrange("p (k e) -> p k e", k=2)[:, :, bass.ds(e, 1)]
                              ).then_inc(S["cols"], 1)
                dve.wait_ge(S["cols"], t + 1)
                v.tensor_copy(du[:, u, :], cd[:, u, 1:2]).then_inc(S["place"], 1)

            def split(t, u):
                dve.wait_ge(S["xa"], t + 1)
                if not below(t, 2):
                    dve.wait_ge(S["hidden_ps"], t - 1)
                v.tensor_copy(xhi[:, u % 2], xa[:, u % 2]).then_inc(S["x_hi"], 1)
                dve.wait_ge(S["x_hi"], t + 1)
                v.tensor_tensor(xlo[:, u % 2], xa[:, u % 2], xhi[:, u % 2].bitcast(f32), ALU.subtract
                                ).then_inc(S["x_lo"], 1)

            def hiddenT(t, u):
                dve.wait_ge(S["hT_ps"], t + 1)
                if not below(t, 2):
                    dve.wait_ge(S["out_ps"], t - 1)
                v.tensor_copy(GT[:, u % 2], PS[:, 4 + u % 2, :]).then_inc(S["hT_sb"], 1)
            slots(dve, TILES, [(2, split), (1, columns), (0, hiddenT)], (columns,))

            def stats_back(k, p):
                if not below(k, UP):
                    dve.wait_ge(S["y3"], k - UP + 1)
                v.tensor_copy(nr3[:, p], kept[:, bass.ds(k, 1)].rearrange("p a n t -> p (a n) t")
                              ).then_inc(S["nr3"], 1)

            def sum3(k, p):
                dve.wait_ge(S[f"in{p}"], 12 * (k - p) + 48)
                v.tensor_tensor(T3[p], RES[p][:, :, 0, :], RES[p][:, :, 1, :], ALU.add).then_inc(S["t3"], 1)

            def sum3y(k, p):
                dve.wait_ge(S["y3"], k + 1)
                dve.wait_ge(S["t3"], 2 * k + 1)
                v.tensor_tensor(T3[p], T3[p], Y3[p], ALU.add).then_inc(S["t3"], 1)

            def stats3(k, p):
                dve.wait_ge(S["t3"], 2 * k + 2)
                stats(T3[p], mv3[:, p], k, S["bn3"], S["stats3"])

            def scale3(k, p):
                dve.wait_ge(S["c3"], k + 1)
                v.tensor_tensor(T3[p], T3[p], outg[:].unsqueeze(1).broadcast_to([R, NT, D]), ALU.mult
                                ).then_inc(S["g3"], 1)

            def output(k, p):
                dve.wait_ge(S["residual3"], k + 1)
                if not below(k, UP):
                    dve.wait_ge(S[f"st{p}"], 8 * (k - p))
                dve.wait_ge(S["g3"], k + 1)
                v.tensor_tensor(fin[p], T3[p], H3[p], ALU.add).then_inc(S["fin"], 1)
            slots(dve, B, [(3, stats_back), (0, sum3), (-2, scale3), (0, sum3y), (-2, output), (0, stats3)])

        @block.tensor
        def _(pe):
            mm, tr = nc.tensor.matmul, nc.tensor.transpose

            def tok(b, t):
                if t == 0:
                    pe.wait_ge(S["x_loaded"], 96 * (b + 1))
                    if below(b, 1):
                        pe.wait_ge(S["tok_weights"], 16)
                        pe.wait_ge(S["setup_vector"], 1)
                    else:
                        pe.wait_ge(S["vb"], b)
                xv = xt[:].rearrange("p (h w q) -> p h w q", w=HP, q=P16)
                for q in range(QH):
                    last = mm(PS[0:R, MA, t * D:(t + 1) * D], xv[:, t * HP // 2:(t + 1) * HP // 2, :, q],
                              wtok[:, q, :], start=(q == 0), stop=(q == QH - 1))
                if t == 1:
                    last.then_inc(S["tok_ps"], 1)

            def xn_T(b):
                pe.wait_ge(S["xn"], b + 1)
                pe.wait_ge(S["h0"], b + 1)
                for t in range(NT):
                    last = tr(PS[:, MA, t * R:(t + 1) * R], xn[:, t, :], idn[0:R, 0:R])
                last.then_inc(S["xnT_ps"], 1)

            def qk(b, n, m):
                if m == 0:
                    pe.wait_ge(S["xnT_sb"], b + 1)
                    if n == 1:
                        pe.wait_ge(S["rope"], 4 * b + 1)
                elif n == 1:
                    pe.wait_ge(S["rope"], 4 * b + 2)
                elif not below(b, 2):
                    pe.wait_ge(S["h1"], b - 1)
                w_ = (2 * n + m) * D
                mm(PS[:, (MA, MB)[m], 0:NP], wqkv[:, w_:w_ + D], xnT[:], start=True, stop=True
                   ).then_inc(S["qk_ps"], 1)

            def vproj(b):
                pe.wait_ge(S["rope"], 4 * b + 3)
                keys = [xnT[:, t * 128:(t + 1) * 128] for t in range(FULL)] + [xnR[:].rearrange("p a n -> p (a n)")]
                for t in range(FULL + 1):
                    last = mm(PS[:, MA, t * D:(t + 1) * D], keys[t], wqkv[:, 4 * D:5 * D], start=True, stop=True)
                last.then_inc(S["v_ps"], 1)

            def scores(i, par, g):
                pe.wait_ge(S["q_lo"], NH * i + g + 1)
                if g == 0:
                    pe.wait_ge(S["k_lo"], i + 1)
                for t in range(NT):
                    n = NT * g + t
                    if not (below(i, 1) and g == 0):
                        pe.wait_ge(S["exp"], NH * NT * i + n - NT + 1)
                    rows = slice(t * R, (t + 1) * R)
                    mm(PS[0:R, t, 0:NV], qhi[:, g % QR, rows], khi[:, par, 0:NV], start=True, stop=False)
                    mm(PS[0:R, t, 0:NV], qhi[:, g % QR, rows], klo[:, par, 0:NV], start=False, stop=False)
                    mm(PS[0:R, t, 0:NV], qlo[:, g % QR, rows], khi[:, par, 0:NV], start=False, stop=True
                       ).then_inc(S["scores_ps"], 1)

            def transposed(n, image_n, src, image):
                if not (below(image, 1) and image_n < 2):
                    pe.wait_ge(S["probsT_sb"], n - 1)
                for t in range(NT):
                    last = tr(PS[:, TB + image_n % 2, t * R:(t + 1) * R], src[:, t, :], idn[0:R, 0:R])
                last.then_inc(S["probsT_ps"], 1)

            def probs_T(i, g):
                pe.wait_ge(S["probs"], NH * i + g + 1)
                for c in range(FULL):
                    transposed(tile_no(i, g, c), tile_no(0, g, c), E[:, g % EB, :, c * 128:(c + 1) * 128], i)

            def rest_T(i, r):
                pe.wait_ge(S["rest"], NH * i + (NH // NR) * (r + 1))
                transposed(rest_no(i, r), rest_no(0, r), ER[:, r], i)

            def weighted(i, g):
                pe.wait_ge(S["probsT_sb"], tile_no(i, g, FULL - 1) + 1)
                pe.wait_ge(S["vp"], NH * i + g + 1)
                if g == 0 and not below(i, 1):
                    pe.wait_ge(S["attn_sb"], i)
                for c in range(FULL):
                    last = mm(acc, VP[:, g, c, :], AT[:, g % 2, c, 0:N], start=(g == 0 and c == 0), stop=False)
                last.then_inc(S["av_ps"], 1)

            def weighted_rest(i, r):
                pe.wait_ge(S["probsT_sb"], rest_no(i, r) + 1)
                pe.wait_ge(S["vp_rest"], NR * i + r + 1)
                mm(acc, VR[:, r, :], ATR[:, r, 0:N], start=False, stop=(r == NR - 1)).then_inc(S["av_rest"], 1)

            def proj(j):
                pe.wait_ge(S["attn_sb"], j + 1)
                if not below(j, 1):
                    pe.wait_ge(S["gate_sb"], j)
                for t in range(NT):
                    last = mm(PS[0:R, MB, t * D:(t + 1) * D], oT[:, t * R:(t + 1) * R], wout[:], start=True, stop=True)
                last.then_inc(S["proj_ps"], 1)

            def x2T_(j, par):
                pe.wait_ge(S["xhat"], j + 1)
                if not below(j, 1):
                    pe.wait_ge(S["pos_read"], j)
                else:
                    pe.wait_ge(S["rope"], 4 * (j + 3))
                for t in range(NT):
                    last = tr(PS[:, MB, t * R:(t + 1) * R], xr[:, par, t, 0:D], idn[0:R, 0:R])
                last.then_inc(S["x2T_ps"], 1)

            def gate(j):
                pe.wait_ge(S["x2T_sb"], j + 1)
                for t in range(NT):
                    last = mm(PS[0:R, MB, t * NE:(t + 1) * NE], x2T[:, t * R:(t + 1) * R], wgate[:],
                              start=True, stop=True)
                last.then_inc(S["gate_ps"], 1)

            def rank(j, emb):
                pe.wait_ge(S["both"], j + 1)
                if emb:
                    pe.wait_ge(S["rope"], 4 * (j + 4))
                elif below(j, B - 1):
                    pe.wait_ge(S["h1"], j + 2)
                m_, z = msb[:].rearrange("p t e -> p (t e)"), NT * NE
                before, every = trb[:, 0, :], trb[:, 1, :]
                mm(PS[0:R, MB, 0:z], before, m_, start=True, stop=False)
                mm(PS[0:R, MB, NE:z], every, m_[:, 0:2 * NE], start=False, stop=False)
                mm(PS[0:R, MB, 2 * NE:z], every, m_[:, 0:NE], start=False, stop=False)
                for t in range(NT):
                    last = mm(PS[0:R, MB, z:z + NE], every, m_[:, t * NE:(t + 1) * NE], start=False,
                              stop=(t == NT - 1))
                last.then_inc(S["rank_ps"], 1)

            tok(0, 0)
            tok(0, 1)
            pe.wait_ge(S["small_weights"], 16)
            xn_T(0)
            pe.wait_ge(S["qkv_weights"], 32)
            for n in range(2):
                for m in range(2):
                    qk(0, n, m)
            vproj(0)

            def step(i, par, has):
                emb = has["emb"]
                for g in range(NH):
                    if has["attn"]:
                        scores(i, par, g)
                    if emb:
                        if g < 2:
                            tok(i + 1, g)
                        if g == 6:
                            vproj(i + 1)
                    head = behind(i, g, 2, has)
                    if head:
                        probs_T(*head)
                    last = behind(i, g, 3, has)
                    if last:
                        weighted(*last)
                    if g in (4, 5) and emb:
                        qk(i + 1, g - 4, 0)
                        qk(i + 1, g - 4, 1)
                    if g == 3 and has["res"]:
                        proj(i - 1)
                    if g == 3 and emb:
                        xn_T(i + 1)
                    if g == 7 and has["rout"]:
                        rank(i - 2, emb)
                    if head and head[1] % 4 == 3:
                        rest_T(head[0], head[1] // 4)
                    if last and last[1] % 4 == 3:
                        weighted_rest(last[0], last[1] // 4)
                    if g == 0 and has["rout"]:
                        x2T_(i - 2, par)
                    if g == 1 and has["rout"]:
                        gate(i - 2)
            steps(pe, step)

            pe.wait_ge(S["table_ready"], 1)
            pe.wait_ge(S["attn_sb"], B)
            pe.wait_ge(S["bias_loaded"], 32)
            pe.wait_ge(S["w2_loaded"], 48)
            pe.wait_ge(S["weights_rounded"], 2)

            def rowsT(t, u):
                pe.wait_ge(S[f"row{u}"], 4 * (t - u) + 16)
                if not below(t, 2):
                    pe.wait_ge(S["xa"], t - 1)
                tr(PS[:, u % 2, 0:D], XB[:, u, 0:D], idn[:]).then_inc(S["xT_ps"], 1)

            def hidden(t, u, e):
                pe.wait_ge(S["x_lo"], t + 1)
                if not below(t, 2):
                    pe.wait_ge(S["gelu"], t - 1)
                cols, o = bass.ds(e * FH, FH), PS[:, 2 + u % 2, :]
                mm(o, xhi[:, u % 2], w1hi[:, cols], start=True, stop=False)
                mm(o, xlo[:, u % 2], w1hi[:, cols], start=False, stop=False)
                mm(o, xhi[:, u % 2], w1lo[:, cols], start=False, stop=False)
                mm(o, ones2[:], b1hl[:, cols], start=False, stop=True).then_inc(S["hidden_ps"], 1)

            def hT(t, u):
                pe.wait_ge(S["gelu"], t + 1)
                if not below(t, 2):
                    pe.wait_ge(S["hT_sb"], t - 1)
                for c in range(FC):
                    last = tr(PS[:, 4 + u % 2, c * 128:(c + 1) * 128], hs[:, u % 2, c * 128:(c + 1) * 128], idn[:])
                last.then_inc(S["hT_ps"], 1)

            def second(t, u, e):
                pe.wait_ge(S["hT_sb"], t + 1)
                if not below(t, 2):
                    pe.wait_ge(S["out_sb"], t - 1)
                o = PS[:, 6 + u % 2, 0:D]
                for c in range(FC):
                    mm(o, GT[:, u % 2, c * 128:(c + 1) * 128], w2s[:, bass.ds(e * FH + c * D, D)],
                       start=(c == 0), stop=False)
                mm(o, ones2[:], b2hl[:, bass.ds(e * D, D)], start=False, stop=True).then_inc(S["out_ps"], 1)
            slots(pe, TILES, [(2, rowsT), (1, hidden), (0, hT), (-1, second)], (hidden, second))


def kernel(x, txt, L0_tok_w, L0_tok_b, L0_attn_w_qkv, L0_attn_b_qkv, L0_attn_w_pre, L0_attn_w_post, L0_attn_w_out,
           L0_attn_b_out, L0_ffn_Wg, L0_ffn_W1, L0_ffn_b1, L0_ffn_W2, L0_ffn_b2, L0_ffn_ln_g, L0_ffn_ln_b,
           L0_ffn_out_g, L0_ffn_out_b):
    import concourse.bacc as bacc
    from concourse.bass_utils import run_bass_kernel_spmd

    def a(v):
        return np.asarray(v)

    f = np.float32
    wtok = np.zeros((KR + 1, QH, D), f)
    wtok[:KR] = a(L0_tok_w).reshape(D, C, P16, 2, QH).transpose(3, 1, 2, 4, 0).reshape(KR, QH, D)
    wtok[KR, 0] = a(L0_tok_b)
    partner = np.arange(D) ^ (DH // 4)
    wq, wk, wv = a(L0_attn_w_qkv).reshape(3, D, D)
    bq, bk, bvv = a(L0_attn_b_qkv).reshape(3, D)
    wqkv = np.concatenate([wq.T, wq[partner].T, wk.T, wk[partner].T, wv.T], axis=1)
    bqk = np.stack([bq, bq[partner], bk, bk[partner]], axis=1)
    inv = (1.0 / f(10000.0) ** (np.arange(0, DH, 4, dtype=f) / f(DH))).astype(f)
    pos = np.arange(NP)
    low, chunk = (pos % 64).astype(f), (pos // 64).astype(f)
    rope = np.zeros((D, 2, NP), f)
    for p in range(D):
        d = p % DH
        ang = (low if d < DH // 2 else chunk) * inv[d % 4]
        rope[p, 0] = np.cos(ang)
        rope[p, 1] = np.sin(ang) * (1 if d & 4 else -1)
    consts = np.zeros((R, 4, NT, NE), f)
    token = np.arange(NT)[None, :] * R + np.arange(R)[:, None]
    consts[:, 0] = consts[:, 1] = (token < N)[:, :, None]
    consts[:, 2] = (np.arange(NE) * REGION)[None, None, :]
    consts[:, 3] = 2 * token[:, :, None]
    tri = np.stack([np.triu(np.ones((R, R), f), 1), np.ones((R, R), f)], axis=1)
    tail = np.zeros((128, ROW), f)
    tail[:, D + NE:] = 4 * B * N
    tile_no = np.arange(TILES, dtype=f)

    def rows(vec, count=R):
        return np.repeat(a(vec)[None, :], count, axis=0)
    post = np.repeat(a(L0_attn_w_post).T, DH, axis=1)
    post_rest = np.repeat(post.reshape(NR, NH // NR, D), RK, axis=1).transpose(1, 0, 2)

    parts = {
        "b_qkr": bqk, "b_v": rows(bvv, 128), "w_pre": np.repeat(a(L0_attn_w_pre).T, DH, axis=0),
        "w_post": np.concatenate([np.repeat(post[None], 128, axis=0), post_rest], axis=1),
        "w_out": a(L0_attn_w_out).T, "b_out": rows(L0_attn_b_out), "w_gate": a(L0_ffn_Wg),
        "ln_g": a(L0_ffn_ln_g)[:, None], "ln_b": a(L0_ffn_ln_b)[:, None],
        "out_g": rows(L0_ffn_out_g), "out_b": rows(L0_ffn_out_b), "ident": np.eye(128, dtype=f),
        "iota": np.repeat(np.arange(NE, dtype=f)[None], R, axis=0), "consts": consts, "tri": tri,
    }
    small = []
    for name, (count, shape) in SMALL.items():
        piece = np.zeros((128, int(np.prod(shape))), f)
        piece[:count] = parts[name].reshape(count, -1)
        small.append(piece)
    arrays = {
        "x": a(x), "txt": a(txt), "w_tok": wtok, "w_qkvr": wqkv, "small": np.concatenate(small, axis=1),
        "w1": a(L0_ffn_W1).transpose(1, 0, 2).reshape(D, NE * FH),
        "b12": np.concatenate([a(L0_ffn_b1).reshape(128, -1), a(L0_ffn_b2).reshape(128, -1)], axis=1),
        "w2": a(L0_ffn_W2).reshape(NE * FC, 128, D).transpose(1, 0, 2).reshape(128, NE * FC * D),
        "rope": rope, "tail": tail, "tiota": np.stack([tile_no, 128 * tile_no])[None],
    }
    nc = bacc.Bacc("TRN2", target_bir_lowering=False, num_devices=1)
    f32 = mybir.dt.float32
    ins, args = {}, []
    for name, v in arrays.items():
        v = np.ascontiguousarray(v)
        ins[f"in_{name}"] = v
        args.append(nc.dram_tensor(f"in_{name}", v.shape, mybir.dt.from_np(v.dtype), kind="ExternalInput").ap())
    for name, shape in (("routed", (DUMMY + 128, ROW)), ("results", (B * N, 2 * D)), ("h1", (B, R, NT * D))):
        args.append(nc.dram_tensor(f"dram_{name}", shape, f32).ap())
    args.append(nc.dram_tensor("dram_bias", (2, NE * (FH + D)), mybir.dt.float32r).ap())
    args.append(nc.dram_tensor("out_0", (B, N, D), f32, kind="ExternalOutput").ap())
    early_fusion_kernel(nc, *args)
    r = run_bass_kernel_spmd(nc, [ins], core_ids=[0])
    return r.results[0]["out_0"]
```
